# Optimizing a Trainium2 kernel written in Bass

```python
import numpy as np
import jax
import jax.numpy as jnp

def _softmax(x, axis=-1):
    return jax.nn.softmax(x, axis=axis)

def _gelu(x):
    return jax.nn.gelu(x, approximate=True)

def _silu(x):
    return jax.nn.silu(x)

def _sigmoid(x):
    return jax.nn.sigmoid(x)

def _layernorm(x, axis=-1, eps=1e-05):
    m = jnp.mean(x, axis=axis, keepdims=True)
    v = jnp.var(x, axis=axis, keepdims=True)
    return (x - m) / jnp.sqrt(v + eps)

def _scatter_add(tgt, idx, src, axis=0):
    return tgt.at[idx].add(src)

def _segment_sum(src, seg, n):
    return jax.ops.segment_sum(src, seg, n)
kernel_name = 'mk_lm_tower_d1_tok_ids1024_r4_47531c'

def setup_inputs(seed: int=0):
    np.random.seed(seed)
    _w = jnp.asarray

    def _rec_inputs():
        import jax
        import jax.numpy as jnp
        _rk = jax.random.key(seed)
        x = jax.random.randint(jax.random.fold_in(_rk, 1), (32, 128), 0, 12564, jnp.int32)
        return x
    x = _rec_inputs()

    def _L0_tok_setup():
        import jax, jax.numpy as jnp
        import numpy as np
        VOCAB = 50257
        DIM = 256
        PADDING_IDX = 0
        key = jax.random.key(seed)
        k_w, k_ids = jax.random.split(key)
        weight = jax.random.normal(k_w, (VOCAB, DIM), dtype=jnp.float32)
        weight = weight.at[PADDING_IDX].set(0.0)
        input_ids = jax.random.randint(k_ids, (16, 512), 0, VOCAB, dtype=jnp.int64)
        return {'weight': weight, 'input_ids': input_ids}
    _L0_tok_all = _L0_tok_setup()
    _L0_tok_in = {k: v for k, v in _L0_tok_all.items() if k in ('weight',)}
    del _L0_tok_all

    def _L0_attn_setup():
        import jax, jax.numpy as jnp
        import numpy as np
        D_MODEL = 256
        NUM_HEADS = 16
        BATCH = 2
        SEQ = 512

        def _trunc_normal(key, shape, std):
            return jax.random.truncated_normal(key, -3.0, 3.0, shape, dtype=jnp.float32) * std
        key = jax.random.key(seed)
        kx, kq, kk, kv, ko = jax.random.split(key, 5)
        std = (2.0 / (D_MODEL + D_MODEL)) ** 0.5
        return {'X': jax.random.normal(kx, (BATCH, SEQ, D_MODEL), dtype=jnp.float32), 'q_proj': _trunc_normal(kq, (D_MODEL, D_MODEL), std), 'k_proj': _trunc_normal(kk, (D_MODEL, D_MODEL), std), 'v_proj': _trunc_normal(kv, (D_MODEL, D_MODEL), std), 'o_proj': _trunc_normal(ko, (D_MODEL, D_MODEL), std)}
    _L0_attn_all = _L0_attn_setup()
    _L0_attn_in = {k: v for k, v in _L0_attn_all.items() if k in ('q_proj', 'k_proj', 'v_proj', 'o_proj')}
    del _L0_attn_all

    def _L0_ffn_setup():
        import jax, jax.numpy as jnp
        import numpy as np
        CAPACITY_FACTOR = 1.25
        key = jax.random.key(seed)
        k1, k2, k3, k4 = jax.random.split(key, 4)
        B, T, D, F, E = (4, 1024, 256, 1024, 8)
        s = 0.02
        return {'x': jax.random.normal(k1, (B, T, D), dtype=jnp.float32), 'wg': jax.random.normal(k2, (D, E), dtype=jnp.float32) * s, 'W1': jax.random.normal(k3, (E, D, F), dtype=jnp.float32) * s, 'b1': jnp.zeros((E, F), dtype=jnp.float32), 'W2': jax.random.normal(k4, (E, F, D), dtype=jnp.float32) * s, 'b2': jnp.zeros((E, D), dtype=jnp.float32)}
    _L0_ffn_all = _L0_ffn_setup()
    _L0_ffn_in = {k: v for k, v in _L0_ffn_all.items() if k in ('wg', 'W1', 'b1', 'W2', 'b2')}
    del _L0_ffn_all
    return {'x': x, 'L0_tok_weight': _L0_tok_in['weight'], 'L0_attn_q_proj': _L0_attn_in['q_proj'], 'L0_attn_k_proj': _L0_attn_in['k_proj'], 'L0_attn_v_proj': _L0_attn_in['v_proj'], 'L0_attn_o_proj': _L0_attn_in['o_proj'], 'L0_ffn_wg': _L0_ffn_in['wg'], 'L0_ffn_W1': _L0_ffn_in['W1'], 'L0_ffn_b1': _L0_ffn_in['b1'], 'L0_ffn_W2': _L0_ffn_in['W2'], 'L0_ffn_b2': _L0_ffn_in['b2']}

def reference(x, L0_tok_weight, L0_attn_q_proj, L0_attn_k_proj, L0_attn_v_proj, L0_attn_o_proj, L0_ffn_wg, L0_ffn_W1, L0_ffn_b1, L0_ffn_W2, L0_ffn_b2):
    import jax
    import jax.numpy as jnp

    def _L0_tok_ref(weight, input_ids):
        import jax, jax.numpy as jnp
        import numpy as np
        VOCAB = 50257
        DIM = 256
        PADDING_IDX = 0
        return jnp.take(weight, input_ids, axis=0)

    def _L0_attn_ref(X, q_proj, k_proj, v_proj, o_proj):
        import jax, jax.numpy as jnp
        import numpy as np
        D_MODEL = 256
        NUM_HEADS = 16
        BATCH = 2
        SEQ = 512

        def _trunc_normal(key, shape, std):
            return jax.random.truncated_normal(key, -3.0, 3.0, shape, dtype=jnp.float32) * std
        B, S, D = X.shape
        H = NUM_HEADS
        d_k = D // H
        q_w = q_proj.reshape(H, d_k, D)
        k_w = k_proj.reshape(H, d_k, D)
        v_w = v_proj.reshape(H, d_k, D)
        o_w = o_proj.reshape(D, H, d_k).transpose(1, 0, 2)
        q = jnp.einsum('hkd,bsd->bhsk', q_w, X)
        k = jnp.einsum('hkd,bsd->bhsk', k_w, X)
        v = jnp.einsum('hkd,bsd->bhsk', v_w, X)
        scale = 1.0 / jnp.sqrt(jnp.asarray(d_k, dtype=X.dtype))
        scores = jnp.einsum('bhqk,bhsk->bhqs', q, k) * scale
        causal = jnp.tril(jnp.ones((S, S), dtype=bool))
        scores = jnp.where(causal, scores, jnp.asarray(-jnp.inf, dtype=scores.dtype))
        attn = jax.nn.softmax(scores, axis=-1)
        attn_out = jnp.einsum('bhqs,bhsk->bhqk', attn, v)
        return jnp.einsum('hdv,bhsv->bsd', o_w, attn_out)

    def _L0_ffn_ref(x, wg, W1, b1, W2, b2):
        import jax, jax.numpy as jnp
        import numpy as np
        CAPACITY_FACTOR = 1.25
        B, T, D = x.shape
        E = wg.shape[1]
        N = B * T
        capacity = int(N / E * CAPACITY_FACTOR) + 1
        xf = x.reshape(N, D)
        logits = xf @ wg
        scores = jax.nn.softmax(logits, axis=-1)
        top1 = jnp.argmax(scores, axis=-1)
        combine_w = jnp.take_along_axis(scores, top1[:, None], axis=1)[:, 0]
        oh = jax.nn.one_hot(top1, E, dtype=jnp.int32)
        rank = jnp.take_along_axis(jnp.cumsum(oh, axis=0), top1[:, None], axis=1)[:, 0] - 1
        valid = rank < capacity
        trash = E * capacity
        slot = jnp.where(valid, top1 * capacity + rank, trash)
        buf = jnp.zeros((E * capacity + 1, D), dtype=x.dtype).at[slot].set(xf)
        eb = buf[:E * capacity].reshape(E, capacity, D)
        h = jax.nn.gelu(jnp.einsum('ecd,edf->ecf', eb, W1) + b1[:, None, :], approximate=False)
        y = jnp.einsum('ecf,efd->ecd', h, W2) + b2[:, None, :]
        yf = y.reshape(E * capacity, D)
        gathered = yf[jnp.minimum(slot, E * capacity - 1)]
        out_flat = jnp.where(valid[:, None], gathered, 0.0) * combine_w[:, None]
        return out_flat.reshape(B, T, D)
    h = _L0_tok_ref(L0_tok_weight, x)
    h = h + _L0_attn_ref(_layernorm(h, axis=-1), L0_attn_q_proj, L0_attn_k_proj, L0_attn_v_proj, L0_attn_o_proj)
    h = h + _L0_ffn_ref(_layernorm(h, axis=-1), L0_ffn_wg, L0_ffn_W1, L0_ffn_b1, L0_ffn_W2, L0_ffn_b2)
    return h

_drawn_inputs = setup_inputs


def setup_inputs(seed=0):
    import zlib

    import numpy as np

    out = dict(_drawn_inputs(seed))
    spreads = {'L0_ffn_b1': (0.0, 0.8), 'L0_ffn_b2': (0.0, 0.423)}
    factors = {'L0_ffn_W1': 2.767}
    for name, (base, spread) in spreads.items():
        noise = np.random.default_rng([zlib.crc32(name.encode()), seed]).standard_normal(out[name].shape)
        drawn = base * np.exp(spread * noise) if base else spread * noise
        out[name] = jnp.asarray(drawn.astype(out[name].dtype))
    for name, factor in factors.items():
        out[name] = (out[name] * factor).astype(out[name].dtype)
    return out
```

```python
from contextlib import ExitStack

import concourse.bass as bass
from concourse import mybir

P = 128
F32 = mybir.dt.float32
F32R = mybir.dt.float32r
BF16 = mybir.dt.bfloat16
U32 = mybir.dt.uint32
I32 = mybir.dt.int32
ALU = mybir.AluOpType
ACT = mybir.ActivationFunctionType
AX_X = mybir.AxisListType.X

EPS = 1e-5
MASKED = -1e30
RING = 3
UNITS = 8
AHEAD = 4
ROW = 260


class Turn:

    def __init__(self, n, off, period):
        self.n, self.off, self.period = n, off, period
        self.slot = off % period

    def times(self, per, more=0):
        base = per * self.off + more
        return base if isinstance(self.n, int) else self.n * (per * self.period) + base

    def round(self, per, more=0):
        base = per * (self.off // self.period) + more
        return base if isinstance(self.n, int) else self.n * per + base

    def back(self, k):
        return Turn(self.n, self.off - k, self.period)


def wait(engine, semaphore, value):
    if isinstance(value, int) and value <= 0:
        return
    engine.wait_ge(semaphore, value)


def hold(engine, semaphore, value):
    wait(engine, semaphore, value)
    if not isinstance(value, int):
        engine.nop(nofuse=True)


def lm_block(nc, x, table, wq, wk, wv, wo, wg, W1, b1, W2, b2, out):
    NB, S = x.shape
    D = table.shape[1]
    E, _, F = W1.shape
    H, DK = 16, D // 16
    N = NB * S
    CAP = int(N / E * 1.25) + 1
    KC = D // P
    GB = 2
    NG = NB // GB
    GT = GB * S
    QUADS = H // 4
    PARTS = 3
    KS_ROWS = 6 * DK
    SCALE = float(DK) ** -0.5
    NT = 6
    TS = -(-CAP // NT)
    TS += TS % 2
    SL = NT * TS
    NH = SL // 2
    FC = F // P
    NOWHERE = 1 << 20
    assert S == P and TS <= P and NH <= 512

    tab = nc.dram_tensor("token_of_slot", [E * SL, 1], U32)
    rows = nc.dram_tensor("h_rows", [N, ROW], F32)
    qparts = [nc.dram_tensor(f"q_parts{i}", [PARTS, D, GT], BF16) for i in range(RING)]
    kparts = [nc.dram_tensor(f"k_parts{i}", [PARTS, D, GT], BF16) for i in range(RING)]
    outf = out.rearrange("b s d -> (b s) d")

    with ExitStack() as whole:
        def sb_in(scope):
            return lambda name, shape, dt: scope.enter_context(nc.sbuf_tensor(name, shape, dt))

        sb = sb_in(whole)

        def sem(name):
            return whole.enter_context(nc.semaphore(name))

        bank = {n: whole.enter_context(nc.psum_tensor(n, [P, 512], F32))
                for n in ("S0", "S1", "C0", "C1", "PV", "M0", "M1", "M2")}
        bS = [bank["S0"], bank["S1"]]
        bC = [bank["C0"], bank["C1"]]
        bPV, bM0, bM1, bM2 = bank["PV"], bank["M0"], bank["M1"], bank["M2"]

        identf = sb("identf", [P, P], F32)
        raw = [sb(f"w_raw{q}", [P, 2 * KC * F], F32) for q in range(2)]
        b1t = sb("b1t", [P, E * FC], F32)
        halfneg = sb("halfneg", [P, 8], F32)
        d_raw = [sem(f"d_raw{q}") for q in range(2)]

        def load_experts(eng, e, q):
            eng.dma_start(raw[q][:, 0:KC * F].rearrange("p (k f) -> p k f", k=KC),
                          W1[bass.ds(e, 1)].rearrange("a (k p) f -> p (a k) f", p=P)).then_inc(d_raw[q], 16)
            eng.dma_start(raw[q][:, KC * F:].rearrange("p (c d) -> p c d", c=FC),
                          W2[bass.ds(e, 1)].rearrange("a (c p) d -> p (a c) d", p=P)).then_inc(d_raw[q], 16)

        attention_phase(nc, sb_in, sem, locals())
        expert_phase(nc, sb_in, sem, locals())


def attention_phase(nc, sb_in, sem, v):
    x, table, wq, wk, wv, wo, wg, b1 = (v[n] for n in ("x", "table", "wq", "wk", "wv", "wo", "wg", "b1"))
    NB, S, D, E, H, DK, CAP, KC, GB, NG, GT, QUADS = (
        v[n] for n in ("NB", "S", "D", "E", "H", "DK", "CAP", "KC", "GB", "NG", "GT", "QUADS"))
    PARTS, KS_ROWS, SCALE, SL, FC, NOWHERE, N = (
        v[n] for n in ("PARTS", "KS_ROWS", "SCALE", "SL", "FC", "NOWHERE", "N"))
    tab, rows, qparts, kparts, outf = (v[n] for n in ("tab", "rows", "qparts", "kparts", "outf"))
    bS, bC, bPV, bM0, bM1, bM2 = (v[n] for n in ("bS", "bC", "bPV", "bM0", "bM1", "bM2"))
    identf, b1t, halfneg, load_experts = (v[n] for n in ("identf", "b1t", "halfneg", "load_experts"))
    BIG = float(NOWHERE)

    with ExitStack() as scope:
        sb = sb_in(scope)
        identb = sb("identb", [P, P], BF16)
        maskb = sb("maskb", [P, S], BF16)
        trib = sb("trib", [P, P], BF16)
        onesb = sb("onesb", [P, P], BF16)
        eps_of = sb("eps_of", [P, GB * E], I32)
        iota8 = sb("iota8", [P, GB, E], F32)
        base = sb("base", [P, E], F32)
        limit = sb("limit", [P, E], F32)
        tid_all = sb("tid_all", [P, NB], U32)
        nowhere = sb("nowhere", [96, E * SL // 96], U32)
        wraw = sb("wraw", [P, 4, KC, D], F32)
        wh = [sb(f"wh{m}", [P, KC, D], F32R) for m in range(4)]
        wl = [sb(f"wl{m}", [P, KC, D], F32R) for m in range(4)]
        wgs = sb("wgs", [P, KC, E], F32)
        b1raw = sb("b1raw", [E * FC, P], F32)
        xi = sb("xi", [NB, S], I32)
        xf = sb("xf", [NB, S], F32)
        idt = sb("idt", [P, NB], U32)
        h = sb("h", [P, NB, ROW], F32)
        st1 = sb("st1", [P, GB, 6], F32)
        mv1 = sb("mv1", [P, GB, 2], F32)
        ve1 = sb("ve1", [P, GB], F32)
        rs1 = sb("rs1", [P, GB], F32)
        xn = sb("xn", [P, GB, D], F32)
        xth = sb("xth", [P, KC, GT], F32R)
        xtl = sb("xtl", [P, KC, GT], F32R)
        qp = sb("qp", [P, PARTS, KC, GT], BF16)
        kp = sb("kp", [P, PARTS, KC, GT], BF16)
        qr = sb("qr", [P, KC, GT], F32)
        kr = sb("kr", [P, KC, GT], F32)
        qs = [sb(f"qs{i}", [KS_ROWS + 1, H, GT], BF16) for i in range(RING)]
        ks = [sb(f"ks{i}", [KS_ROWS + 1, H, GT], BF16) for i in range(RING)]
        va = [sb(f"va{i}", [P, GB, H, 2 * DK], F32) for i in range(RING)]
        mx = [sb(f"mx{i}", [P, GB * H], F32) for i in range(RING)]
        nm = [sb(f"nm{i}", [GB * H, S], BF16) for i in range(RING)]
        pt = [sb(f"pt{i}", [P, 4, S], F32) for i in range(4)]
        osb = [sb(f"os{i}", [P, QUADS, S], F32) for i in range(GB)]
        rec = sb("rec", [P, GB, H], F32)
        on = sb("on", [P, GB, D], F32)
        oth = sb("oth", [P, KC, GT], F32R)
        otl = sb("otl", [P, KC, GT], F32R)
        st2 = sb("st2", [P, GB, 6], F32)
        mv2 = sb("mv2", [P, GB, 2], F32)
        ve2 = sb("ve2", [P, GB], F32)
        rs2 = sb("rs2", [P, GB], F32)
        xn2 = sb("xn2", [P, GB, D], F32)
        x2t = sb("x2t", [P, KC, GT], F32)
        lmax = sb("lmax", [P, GB], F32)
        leq = sb("leq", [P, GB, E], F32)
        first = sb("first", [P, GB], F32)
        oh = sb("oh", [P, GB, E], BF16)
        dl = sb("dl", [P, GB, E], F32)
        ex = sb("ex", [P, GB, E], F32)
        se = sb("se", [P, GB], F32)
        cn = sb("cn", [P, GB, E], F32)
        over = sb("over", [P, GB, E], F32)
        pl = sb("pl", [P, GB, E], F32)
        pm = sb("pm", [P, GB, E], F32)
        pos = sb("pos", [P, GB], U32)
        tid = sb("tid", [P, GB], U32)

        d_x, d_w, d_c, d_init = sem("d_x"), sem("d_w"), sem("d_c"), sem("d_init")
        d_g = [sem(f"d_g{i}") for i in range(RING)]
        d_qw, d_kw = sem("d_qw"), sem("d_kw")
        d_q = [sem(f"d_q{i}") for i in range(RING)]
        d_k = [sem(f"d_k{i}") for i in range(RING)]
        d_sh = [sem(f"d_sh{i}") for i in range(RING)]
        d_rows, d_tab = sem("d_rows"), sem("d_tab")
        g_set, g_cst, v_cst = sem("g_set"), sem("g_cst"), sem("v_cst")
        v_xf, pe_id, v_idt, pe_w, a_wh, v_wl = (sem(n) for n in ("v_xf", "pe_id", "v_idt", "pe_w", "a_wh", "v_wl"))
        pe_b1, v_b1 = sem("pe_b1"), sem("v_b1")
        pe_T, pe_Q, pe_K, pe_V, pe_S, pe_mT, pe_C, pe_PV, pe_OT, pe_oT, pe_O, pe_x2T, pe_lg, pe_rk = (
            sem("pe_" + n) for n in ("T", "Q", "K", "V", "S", "mT", "C", "PV", "OT", "oT", "O", "x2T", "lg", "rk"))
        a_xth, a_q1, a_q2, a_k1, a_k2, a_V, a_exp, a_nm, a_os, a_oth, a_x2t, a_ex = (
            sem("a_" + n) for n in ("xth", "q1", "q2", "k1", "k2", "V", "exp", "nm", "os", "oth", "x2t", "ex"))
        v_st1, v_mv1, v_ve1, v_xn, v_xtl, v_qr, v_kr, v_mx, v_rec, v_on, v_otl = (
            sem("v_" + n) for n in ("st1", "mv1", "ve1", "xn", "xtl", "qr", "kr", "mx", "rec", "on", "otl"))
        v_h1, v_st2, v_mv2, v_ve2, v_xn2, v_lmax, v_leq, v_first, v_dl, v_se, v_w = (
            sem("v_" + n) for n in ("h1", "st2", "mv2", "ve2", "xn2", "lmax", "leq", "first", "dl", "se", "w"))
        v_oh, v_cn, v_over, v_pl, v_pm, v_base, v_tid, v_pos = (
            sem("v_" + n) for n in ("oh", "cn", "over", "pl", "pm", "base", "tid", "pos"))
        p_q3, p_k3, p_sel, p_rs1, p_rs2 = (sem("p_" + n) for n in ("q3", "k3", "sel", "rs1", "rs2"))

        def group(n, off):
            if isinstance(n, int) and not 0 <= off < NG:
                return None
            return Turn(n, off, RING)

        FIRST = AHEAD + 1
        ROUNDS = (NG - 1 - FIRST) // RING
        AFTER = FIRST + RING * ROUNDS
        LAST = NG + AHEAD

        def steps(eng, step):
            for i in range(FIRST):
                step(0, i)
            with eng.Fori(0, ROUNDS) as n:
                for c in range(RING):
                    step(n, FIRST + c)
            for i in range(AFTER, LAST):
                step(0, i)

        def shift_unit(n, i, s, lag):
            d, u = divmod(s - lag, UNITS)
            return group(n, i + d), u

        C_LAG, PV_LAG = 2 * UNITS + 3, 2 * UNITS + 5

        block = scope.enter_context(nc.Block())

        @block.sync
        def _(sp):
            sp.dma_start(xi[:, :], x).then_inc(d_x, 16)
            for m, w in enumerate((wq, wk, wv, wo)):
                sp.dma_start(wraw[:, m], w.rearrange("(c p) d -> p c d", p=P)).then_inc(d_w, 16)
            sp.dma_start(wgs[:, :, :], wg.rearrange("(k p) e -> p k e", p=P)).then_inc(d_c, 16)
            sp.dma_start(b1raw[:, :], b1.rearrange("e (c p) -> (e c) p", p=P)).then_inc(d_c, 16)
            sp.wait_ge(g_set, 1)
            sp.dma_start(tab[:, :].rearrange("(p n) o -> p (n o)", p=96), nowhere[:, :]).then_inc(d_init, 16)
            load_experts(sp, 0, 0)
            load_experts(sp, 1, 1)

            def stacks(parts, stacked, order, done):
                for c, part in enumerate(order):
                    sp.dma_start(stacked[c * DK:(c + 1) * DK, :, :],
                                 parts[part].rearrange("(h d) t -> d h t", d=DK)).then_inc(done, 16)

            def step(n, i):
                g = group(n, i - 2)
                if g:
                    hold(sp, a_nm, g.times(1, 1))
                    hold(sp, pe_C, g.back(2).times(UNITS))
                    for b in range(GB):
                        sp.dma_start(qs[g.slot][KS_ROWS:KS_ROWS + 1, :, b * S:(b + 1) * S],
                                     nm[g.slot][b * H:(b + 1) * H, :]).then_inc(d_sh[g.slot], 16)
                g = group(n, i)
                if g:
                    hold(sp, pe_C, g.back(2).times(UNITS))
                    hold(sp, p_q3, g.times(1, 1))
                    sp.dma_start(qparts[g.slot][:, :, :].rearrange("a (k p) t -> p (a k) t", p=P),
                                 qp[:, :, :, :].rearrange("p a k t -> p (a k) t")).then_inc(d_qw, 16)
                    hold(sp, p_k3, g.times(1, 1))
                    sp.dma_start(kparts[g.slot][:, :, :].rearrange("a (k p) t -> p (a k) t", p=P),
                                 kp[:, :, :, :].rearrange("p a k t -> p (a k) t")).then_inc(d_kw, 16)
                    hold(sp, d_qw, g.times(16, 16))
                    stacks(qparts[g.slot], qs[g.slot], (0, 0, 1, 1, 0, 2), d_q[g.slot])
                    hold(sp, d_kw, g.times(16, 16))
                    stacks(kparts[g.slot], ks[g.slot], (0, 1, 0, 1, 2, 0), d_k[g.slot])
                g = group(n, i - 4)
                if g:
                    hold(sp, v_w, g.times(1, 1))
                    hg = h[:, bass.ds(g.times(GB), GB), :]
                    sp.dma_start(rows[bass.ds(g.times(GT), GT), :].rearrange("(b p) c -> p b c", p=P),
                                 hg).then_inc(d_rows, 16)
                    sp.dma_start(outf[bass.ds(g.times(GT), GT), :].rearrange("(b p) c -> p b c", p=P),
                                 hg[:, :, 0:D]).then_inc(d_rows, 16)

            steps(sp, step)
            sp.wait_ge(d_rows, 32 * NG)
            sp.wait_ge(d_tab, 32 * NG)

        @block.gpsimd
        def _(pool):
            pool.memset(identf[:, :], 0.0).then_inc(g_cst, 1)
            pool.memset(nowhere[:, :], NOWHERE).then_inc(g_set, 1)
            pool.memset(maskb[:, :], 0.0).then_inc(g_cst, 1)
            pool.memset(trib[:, :], 1.0).then_inc(g_cst, 1)
            pool.wait_ge(g_cst, 3)
            pool.affine_select(out=identf[:, :], in_=identf[:, :], compare_op=ALU.not_equal, fill=1.0, base=0,
                               pattern=[[-1, P]], channel_multiplier=1).then_inc(g_set, 1)
            pool.affine_select(out=maskb[:, :], in_=maskb[:, :], compare_op=ALU.is_ge, fill=MASKED, base=0,
                               pattern=[[-1, S]], channel_multiplier=1).then_inc(g_set, 1)
            pool.affine_select(out=trib[:, :], in_=trib[:, :], compare_op=ALU.is_ge, fill=0.0, base=0,
                               pattern=[[1, P]], channel_multiplier=-1).then_inc(g_set, 1)
            pool.iota(eps_of[:, :], pattern=[[0, GB], [1, E]], base=0, channel_multiplier=0).then_inc(g_set, 1)
            pool.iota(tid_all[:, :], pattern=[[P, NB]], base=0, channel_multiplier=1).then_inc(g_set, 1)

            def gather(g):
                wait(pool, d_g[g % RING], 16 * GB * (g // RING))
                for b in range(GB * g, GB * g + GB):
                    pool.indirect_dma_start(out=h[:, b, 0:D], out_offset=None, in_=table,
                                            in_offset=bass.IndirectOffsetOnAxis(ap=idt[:, b:b + 1], axis=0)
                                            ).then_inc(d_g[g % RING], 16)

            gathers = list(range(NG))
            pool.wait_ge(v_idt, 1)
            for g in gathers[:2]:
                gather(g)
            del gathers[:2]
            pool.wait_ge(v_cst, 4)
            pool.wait_ge(v_ve1, 1)
            pool.tensor_tensor(rs1[:, :], ve1[:, :], halfneg[:, 0:GB], ALU.pow).then_inc(p_rs1, 1)
            for g in gathers[:1]:
                gather(g)
            del gathers[:1]

            def step(n, i):
                for s in range(UNITS):
                    g, u = shift_unit(n, i, s, C_LAG)
                    if g:
                        buf = pt[u % 4]
                        hold(pool, a_exp, g.times(UNITS, u + 1))
                        pool.affine_select(out=buf[:, :, :], in_=buf[:, :, :], compare_op=ALU.is_ge, fill=0.0,
                                           base=0, pattern=[[0, 4], [1, S]], channel_multiplier=-1
                                           ).then_inc(p_sel, 1)
                    g = group(n, i - 4)
                    if g and s == 2:
                        wait(pool, v_ve2, g.times(1, 1))
                        pool.tensor_tensor(rs2[:, :], ve2[:, :], halfneg[:, 0:GB], ALU.pow).then_inc(p_rs2, 1)
                    g = group(n, i)
                    if g and s == 2:
                        wait(pool, a_q2, g.times(1, 1))
                        pool.tensor_tensor(qp[:, 2], qr[:, :, :], qp[:, 1], ALU.subtract).then_inc(p_q3, 1)
                    if g and s == 3:
                        wait(pool, a_k2, g.times(1, 1))
                        pool.tensor_tensor(kp[:, 2], kr[:, :, :], kp[:, 1], ALU.subtract).then_inc(p_k3, 1)
                    g = group(n, i + 1)
                    if g and s == 5:
                        wait(pool, v_ve1, g.times(1, 1))
                        pool.tensor_tensor(rs1[:, :], ve1[:, :], halfneg[:, 0:GB], ALU.pow).then_inc(p_rs1, 1)
                    if isinstance(n, int) and gathers and s in (1, 2, 4, 6):
                        gather(gathers.pop(0))
                g = group(n, i - 4)
                if g:
                    if g.off == 0:
                        wait(pool, d_init, 16)
                    hold(pool, v_tid, g.times(1, 1))
                    hold(pool, v_pos, g.times(1, 1))
                    for b in range(GB):
                        pool.indirect_dma_start(out=tab[:, :],
                                                out_offset=bass.IndirectOffsetOnAxis(ap=pos[:, b:b + 1], axis=0),
                                                in_=tid[:, b:b + 1], in_offset=None,
                                                bounds_check=E * SL - 1, oob_is_err=False).then_inc(d_tab, 16)

            steps(pool, step)

        @block.scalar
        def _(act):
            for m in range(4):
                act.wait_ge(pe_w, m + 1)
                act.activation(wh[m][:, :, :], [bM1, bM2, bS[0], bS[1]][m][:, :].rearrange("p (k d) -> p k d", k=KC),
                               ACT.Copy).then_inc(a_wh, 1)

            def step(n, i):
                for s in range(UNITS):
                    g, u = shift_unit(n, i, s, C_LAG)
                    if g:
                        wait(act, pe_C, g.times(UNITS, u + 1))
                        wait(act, pe_PV, g.times(UNITS, u - 3))
                        act.activation(pt[u % 4][:, :, :], bC[u % 2][:, :].rearrange("p (j t) -> p j t", j=4),
                                       ACT.Exp, scale=SCALE).then_inc(a_exp, 1)
                    g = group(n, i)
                    if g and s == 0:
                        wait(act, pe_T, g.times(1, 1))
                        act.activation(xth[:, :, :], bM0[:, :].rearrange("p (k t) -> p k t", k=KC),
                                       ACT.Copy).then_inc(a_xth, 1)
                    if g and s in (2, 3):
                        done, src, parts, rest, w_done, first_done, rest_done, second_done, third_done = (
                            (pe_Q, bM0, qp, qr, d_qw, a_q1, v_qr, a_q2, p_q3) if s == 2 else
                            (pe_K, bM2, kp, kr, d_kw, a_k1, v_kr, a_k2, p_k3))
                        wait(act, done, g.times(1, 1))
                        wait(act, w_done, g.times(16))
                        act.activation(parts[:, 0], src[:, :].rearrange("p (k t) -> p k t", k=KC),
                                       ACT.Copy).then_inc(first_done, 1)
                    if g and s == 4:
                        wait(act, pe_V, g.times(1, 1))
                        wait(act, pe_PV, g.back(2).times(UNITS))
                        act.activation(va[g.slot][:, :, :, 0:DK].rearrange("p b h d -> p (b h) d"),
                                       bM0[:, :].rearrange("p (c d) -> p c d", d=DK), ACT.Copy).then_inc(a_V, 1)
                    if g and s in (2, 3):
                        wait(act, rest_done, g.times(1, 1))
                        act.activation(parts[:, 1], rest[:, :, :], ACT.Copy).then_inc(second_done, 1)
                    g = group(n, i - 2)
                    if g and s == 0:
                        wait(act, pe_mT, g.times(1, 1))
                        act.activation(nm[g.slot][:, :], bM2[0:GB * H, 0:S], ACT.Copy, scale=-1.0).then_inc(a_nm, 1)
                    g = group(n, i - 3)
                    if g and s in (0, 4):
                        b = s // 4
                        wait(act, pe_PV, g.times(UNITS, 4 * b + 4))
                        act.activation(osb[b][:, :, :], bPV[:, :].rearrange("p (a t) -> p a t", a=QUADS),
                                       ACT.Copy).then_inc(a_os, 1)
                    if g and s == 7:
                        wait(act, pe_oT, g.times(1, 1))
                        act.activation(oth[:, :, :], bM1[:, :].rearrange("p (k t) -> p k t", k=KC),
                                       ACT.Copy).then_inc(a_oth, 1)
                    g = group(n, i - 4)
                    if g and s == 4:
                        wait(act, pe_x2T, g.times(1, 1))
                        act.activation(x2t[:, :, :], bM1[:, :].rearrange("p (k t) -> p k t", k=KC),
                                       ACT.Copy).then_inc(a_x2t, 1)
                    if g and s == 5:
                        wait(act, v_dl, g.times(1, 1))
                        act.activation(ex[:, :, :], dl[:, :, :], ACT.Exp).then_inc(a_ex, 1)

            steps(act, step)

        @block.tensor
        def _(pe):
            pe.wait_ge(g_set, 2)
            pe.wait_ge(v_xf, 1)
            pe.transpose(bM0[:, 0:NB], xf[:, :], identf[0:NB, 0:NB]).then_inc(pe_id, 1)
            pe.wait_ge(d_w, 64)
            for m in range(4):
                dst = [bM1, bM2, bS[0], bS[1]][m]
                for k in range(KC):
                    for c in range(KC):
                        last = pe.transpose(dst[:, k * D + c * P:k * D + (c + 1) * P],
                                            wraw[:, m, c, k * P:(k + 1) * P], identf[:, :])
                last.then_inc(pe_w, 1)
            pe.wait_ge(d_c, 32)
            pe.transpose(bC[0][:, 0:E * FC], b1raw[:, :], identf[0:E * FC, 0:E * FC]).then_inc(pe_b1, 1)
            pe.wait_ge(a_wh, 4)
            pe.wait_ge(v_wl, 4)
            pe.wait_ge(v_idt, 1)
            pe.wait_ge(v_b1, 1)
            pe.wait_ge(v_cst, 10)
            pe.wait_ge(g_set, 6)

            def passes(dst, lhs, rhs, last_of=None):
                pairs = [(a, b) for k in range(KC) for a, b in ((0, 0), (0, 1), (1, 0))]
                for m, (a, b) in enumerate(pairs):
                    k = m // 3
                    last = pe.matmul(dst, lhs[a](k), rhs[b](k), start=(m == 0), stop=(m == len(pairs) - 1))
                return last

            def turn4(dst, src):
                for k in range(KC):
                    for b in range(GB):
                        at = (k * GB + b) * P
                        last = pe.transpose(dst[:, at:at + P], src[:, b, k * P:(k + 1) * P], identf[:, :])
                return last

            def step(n, i):
                for s in range(UNITS):
                    g, u = group(n, i - 1), s
                    if g:
                        if u == 0:
                            wait(pe, d_q[g.slot], g.round(96, 96))
                            wait(pe, d_k[g.slot], g.round(96, 96))
                        dst, b = bS[u % 2], u // QUADS
                        wait(pe, v_mx, g.times(UNITS, u - 1))
                        for j in range(4):
                            hh = (u % QUADS) * 4 + j
                            pe.matmul(dst[:, j * S:(j + 1) * S], identb[:, :], maskb[:, :], start=True, stop=False)
                            last = pe.matmul(dst[:, j * S:(j + 1) * S],
                                             qs[g.slot][0:KS_ROWS, hh, b * S:(b + 1) * S],
                                             ks[g.slot][0:KS_ROWS, hh, b * S:(b + 1) * S],
                                             start=False, stop=True)
                        last.then_inc(pe_S, 1)
                    g, u = shift_unit(n, i, s, C_LAG)
                    if g:
                        if u == 0:
                            wait(pe, d_sh[g.slot], g.round(32, 32))
                        b = u // QUADS
                        wait(pe, a_exp, g.times(UNITS, u - 1))
                        for j in range(4):
                            hh = (u % QUADS) * 4 + j
                            last = pe.matmul(bC[u % 2][:, j * S:(j + 1) * S],
                                             ks[g.slot][:, hh, b * S:(b + 1) * S],
                                             qs[g.slot][:, hh, b * S:(b + 1) * S], start=True, stop=True)
                        last.then_inc(pe_C, 1)
                    g = group(n, i)
                    if g and s == 0:
                        wait(pe, v_xn, g.times(1, 1))
                        wait(pe, a_V, g.times(1))
                        wait(pe, v_on, g.back(4).times(GB, GB))
                        turn4(bM0, xn).then_inc(pe_T, 1)
                    if g and s == 2:
                        wait(pe, a_xth, g.times(1, 1))
                        wait(pe, v_xtl, g.times(1, 1))
                        for c in range(KC):
                            last = passes(bM0[:, c * GT:(c + 1) * GT],
                                          [lambda k, w=w, c=c: w[0][:, k, c * P:(c + 1) * P] for w in (wh, wl)],
                                          [lambda k, t=t: t[:, k, :] for t in (xth, xtl)])
                        last.then_inc(pe_Q, 1)
                    if g and s == 3:
                        wait(pe, v_kr, g.times(1))
                        wait(pe, a_nm, g.back(2).times(1, 1))
                        wait(pe, v_on, g.back(3).times(GB, 1))
                        for c in range(KC):
                            last = passes(bM2[:, c * GT:(c + 1) * GT],
                                          [lambda k, w=w, c=c: w[1][:, k, c * P:(c + 1) * P] for w in (wh, wl)],
                                          [lambda k, t=t: t[:, k, :] for t in (xth, xtl)])
                        last.then_inc(pe_K, 1)
                    if g and s == 4:
                        wait(pe, a_q1, g.times(1, 1))
                        wait(pe, v_qr, g.times(1, 1))
                        for b in range(GB):
                            last = passes(bM0[:, b * D:(b + 1) * D],
                                          [lambda k, t=t, b=b: t[:, k, b * S:(b + 1) * S] for t in (xth, xtl)],
                                          [lambda k, w=w: w[2][:, k, :] for w in (wh, wl)])
                        last.then_inc(pe_V, 1)
                    g = group(n, i - 2)
                    if g and s == 0:
                        wait(pe, v_mx, g.times(UNITS, UNITS))
                        wait(pe, v_kr, g.times(1, 2) if group(n, i - 1) else NG)
                        wait(pe, v_base, g.back(3).times(1, 2))
                        pe.transpose(bM2[0:GB * H, 0:S], mx[g.slot][:, :], identf[:, :]).then_inc(pe_mT, 1)
                    g = group(n, i - 3)
                    if g and s in (1, 6):
                        b = s // 6
                        if b == 0:
                            wait(pe, a_nm, g.times(1, 2) if group(n, i - 2) else NG)
                            wait(pe, v_base, g.back(2).times(1, 2))
                        else:
                            wait(pe, a_V, g.times(1, 4) if group(n, i) else NG)
                            wait(pe, v_on, g.times(GB))
                        wait(pe, a_os, g.times(GB, b + 1))
                        for a in range(QUADS):
                            last = pe.transpose((bM0 if b else bM2)[:, a * P:(a + 1) * P], osb[b][:, a, :],
                                                identf[:, :])
                        last.then_inc(pe_OT, 1)
                    g = group(n, i - 4)
                    if g and s == 0:
                        wait(pe, a_oth, g.times(1, 1))
                        wait(pe, v_otl, g.times(1, 1))
                        for b in range(GB):
                            last = passes(bM1[:, b * D:(b + 1) * D],
                                          [lambda k, t=t, b=b: t[:, k, b * S:(b + 1) * S] for t in (oth, otl)],
                                          [lambda k, w=w: w[3][:, k, :] for w in (wh, wl)])
                        last.then_inc(pe_O, 1)
                    if g and s == 4:
                        wait(pe, v_h1, g.times(1, 1))
                        wait(pe, v_xn2, g.times(1, 1))
                        turn4(bM1, xn2).then_inc(pe_x2T, 1)
                    if g and s == 5:
                        wait(pe, a_x2t, g.times(1, 1))
                        for b in range(GB):
                            for k in range(KC):
                                last = pe.matmul(bM1[:, b * E:(b + 1) * E], x2t[:, k, b * S:(b + 1) * S],
                                                 wgs[:, k, :], start=(k == 0), stop=(k == KC - 1))
                        last.then_inc(pe_lg, 1)
                    g = group(n, i - 3)
                    if g and s == 7:
                        wait(pe, v_on, g.times(GB, GB))
                        wait(pe, v_dl, g.times(1))
                        turn4(bM1, on).then_inc(pe_oT, 1)
                    g = group(n, i - 4)
                    if g and s == 7:
                        wait(pe, v_oh, g.times(1, 1))
                        wait(pe, a_k1, g.times(1, 5) if group(n, i) else NG)
                        wait(pe, v_kr, g.times(1, 5) if group(n, i) else NG)
                        wait(pe, v_on, g.times(GB, GB + 1) if group(n, i - 3) else GB * NG)
                        wait(pe, v_base, g.times(1, 1))
                        pe.matmul(bM2[:, 0:E], trib[:, :], oh[:, 0, :], start=True, stop=True)
                        pe.matmul(bM2[:, E:2 * E], trib[:, :], oh[:, 1, :], start=True, stop=False)
                        pe.matmul(bM2[:, E:2 * E], onesb[:, :], oh[:, 0, :], start=False, stop=True)
                        pe.matmul(bM2[:, 2 * E:3 * E], onesb[:, :], oh[:, 0, :], start=True, stop=False)
                        pe.matmul(bM2[:, 2 * E:3 * E], onesb[:, :], oh[:, 1, :], start=False, stop=True
                                  ).then_inc(pe_rk, 1)
                    g, u = shift_unit(n, i, s, PV_LAG)
                    if g:
                        b = u // QUADS
                        if u == 0:
                            wait(pe, a_V, g.times(1, 1))
                        if u % QUADS == 0:
                            wait(pe, a_os, g.times(GB, b))
                        wait(pe, p_sel, g.times(UNITS, u + 1))
                        for j in range(4):
                            hh = (u % QUADS) * 4 + j
                            last = pe.matmul(bPV[32 * j:32 * j + 32, (u % QUADS) * S:(u % QUADS + 1) * S],
                                             va[g.slot][:, b, hh, :], pt[u % 4][:, j, :], start=True, stop=True)
                        last.then_inc(pe_PV, 1)

            steps(pe, step)

        @block.vector
        def _(dve):
            dve.wait_ge(d_x, 16)
            dve.tensor_copy(xf[:, :], xi[:, :]).then_inc(v_xf, 1)
            dve.memset(halfneg[:, :], -0.5).then_inc(v_cst, 1)
            dve.memset(onesb[:, :], 1.0).then_inc(v_cst, 1)
            dve.memset(h[:, :, D:ROW], 0.0).then_inc(v_cst, 1)
            dve.wait_ge(g_set, 2)
            dve.tensor_copy(identb[:, :], identf[:, :]).then_inc(v_cst, 1)
            dve.wait_ge(pe_id, 1)
            dve.tensor_copy(idt[:, :], bM0[:, 0:NB]).then_inc(v_idt, 1)
            for i in range(RING):
                dve.memset(ks[i][KS_ROWS:KS_ROWS + 1, :, :], 1.0).then_inc(v_cst, 1)
            for i in range(RING):
                last = dve.memset(va[i][:, :, :, DK:2 * DK], 1.0)
            last.then_inc(v_cst, 1)
            dve.wait_ge(g_set, 6)
            dve.tensor_scalar(iota8[:, :, :], eps_of[:, :].rearrange("p (b e) -> p b e", b=GB), -float(E), None,
                              ALU.add).then_inc(v_cst, 1)
            dve.tensor_scalar(base[:, :], eps_of[:, 0:E], float(SL), -1.0, ALU.mult, ALU.add).then_inc(v_base, 1)
            dve.tensor_scalar(limit[:, :], eps_of[:, 0:E], float(SL), float(CAP - 1), ALU.mult, ALU.add
                              ).then_inc(v_cst, 1)
            for m in range(4):
                dve.wait_ge(a_wh, m + 1)
                dve.tensor_tensor(wl[m][:, :, :],
                                  [bM1, bM2, bS[0], bS[1]][m][:, :].rearrange("p (k d) -> p k d", k=KC),
                                  wh[m][:, :, :].bitcast(F32), ALU.subtract).then_inc(v_wl, 1)
            dve.wait_ge(pe_b1, 1)
            dve.tensor_copy(b1t[:, :], bC[0][:, 0:E * FC]).then_inc(v_b1, 1)
            dve.wait_ge(v_cst, 10)

            def stats(g, st, mv, ve, s_st, s_mv, s_ve):
                for b in range(GB):
                    last = dve.bn_stats(st[:, b, :], h[:, bass.ds(g.times(GB, b), 1), 0:D].rearrange("p a d -> p (a d)"))
                last.then_inc(s_st, 1)
                hold(dve, s_st, g.times(1, 1))
                for b in range(GB):
                    last = dve.bn_aggr(mv[:, b, :], st[:, b, :])
                last.then_inc(s_mv, 1)
                wait(dve, s_mv, g.times(1, 1))
                dve.tensor_scalar(ve[:, :], mv[:, :, 1], EPS, None, ALU.add).then_inc(s_ve, 1)

            def normalise(g, dst, mv, rs, done):
                for b in range(GB):
                    last = dve.tensor_scalar(dst[:, b, :],
                                             h[:, bass.ds(g.times(GB, b), 1), 0:D].rearrange("p a d -> p (a d)"),
                                             mv[:, b, 0:1], rs[:, b:b + 1], ALU.subtract, ALU.mult)
                last.then_inc(done, 1)

            def stats1(g):
                wait(dve, d_g[g.slot], g.round(16 * GB, 16 * GB))
                hold(dve, v_xn, g.times(1))
                stats(g, st1, mv1, ve1, v_st1, v_mv1, v_ve1)

            def norm1(g):
                wait(dve, p_rs1, g.times(1, 1))
                normalise(g, xn, mv1, rs1, v_xn)

            g0 = group(0, 0)
            stats1(g0)
            norm1(g0)

            def step(n, i):
                for s in range(UNITS):
                    g, u = group(n, i - 1), s
                    if g:
                        wait(dve, pe_S, g.times(UNITS, u + 1))
                        dve.tensor_reduce(mx[g.slot][:, 4 * u:4 * u + 4],
                                          bS[u % 2][:, :].rearrange("p (j t) -> p j t", j=4), AX_X, ALU.max
                                          ).then_inc(v_mx, 1)
                    g = group(n, i)
                    if g and s == 0:
                        wait(dve, a_xth, g.times(1, 1))
                        dve.tensor_tensor(xtl[:, :, :], bM0[:, :].rearrange("p (k t) -> p k t", k=KC),
                                          xth[:, :, :].bitcast(F32), ALU.subtract).then_inc(v_xtl, 1)
                    if g and s in (2, 3):
                        src, parts, rest, first_done, third_done, rest_done = (
                            (bM0, qp, qr, a_q1, p_q3, v_qr) if s == 2 else (bM2, kp, kr, a_k1, p_k3, v_kr))
                        wait(dve, first_done, g.times(1, 1))
                        wait(dve, third_done, g.times(1))
                        dve.tensor_tensor(rest[:, :, :], src[:, :].rearrange("p (k t) -> p k t", k=KC), parts[:, 0],
                                          ALU.subtract).then_inc(rest_done, 1)
                    g = group(n, i - 4)
                    if g and s == 0:
                        wait(dve, pe_O, g.times(1, 1))
                        hg = h[:, bass.ds(g.times(GB), GB), 0:D]
                        dve.tensor_tensor(hg, bM1[:, :].rearrange("p (b d) -> p b d", b=GB), hg, ALU.add
                                          ).then_inc(v_h1, 1)
                    if g and s == 1:
                        wait(dve, v_h1, g.times(1, 1))
                        hold(dve, v_xn2, g.times(1))
                        stats(g, st2, mv2, ve2, v_st2, v_mv2, v_ve2)
                    if g and s == 3:
                        wait(dve, p_rs2, g.times(1, 1))
                        normalise(g, xn2, mv2, rs2, v_xn2)
                    if g and s == 5:
                        route(g)
                    g = group(n, i + 1)
                    if g and s == 4:
                        stats1(g)
                    if g and s == 6:
                        norm1(g)
                    g = group(n, i - 3)
                    if g and s in (1, 6):
                        b = s // 6
                        src = (bM0 if b else bM2)[:, :].rearrange("p (h c) -> p h c", h=H)
                        wait(dve, pe_OT, g.times(GB, b + 1))
                        dve.reciprocal(rec[:, b, :], src[:, :, DK]).then_inc(v_rec, 1)
                        wait(dve, v_rec, g.times(GB, b + 1))
                        dve.tensor_tensor(on[:, b, :].rearrange("p (h d) -> p h d", h=H), src[:, :, 0:DK],
                                          rec[:, b, :].unsqueeze(2).to_broadcast([P, H, DK]), ALU.mult
                                          ).then_inc(v_on, 1)
                    if g and s == 7:
                        wait(dve, a_oth, g.times(1, 1))
                        dve.tensor_tensor(otl[:, :, :], bM1[:, :].rearrange("p (k t) -> p k t", k=KC),
                                          oth[:, :, :].bitcast(F32), ALU.subtract).then_inc(v_otl, 1)
                    g = group(n, i - 4)
                    if g and s == 7:
                        place(g)

            def spread(t):
                return t[:, :].unsqueeze(2).to_broadcast([P, GB, E])

            def route(g):
                lg = bM1[:, 0:GB * E].rearrange("p (b e) -> p b e", b=GB)
                wait(dve, pe_lg, g.times(1, 1))
                dve.tensor_reduce(lmax[:, :], lg, AX_X, ALU.max).then_inc(v_lmax, 1)
                wait(dve, v_lmax, g.times(1, 1))
                dve.tensor_tensor(leq[:, :, :], lg, spread(lmax), ALU.is_equal).then_inc(v_leq, 1)
                dve.tensor_tensor(dl[:, :, :], lg, spread(lmax), ALU.subtract).then_inc(v_dl, 1)
                wait(dve, v_leq, g.times(2, 1))
                dve.tensor_tensor(leq[:, :, :], leq[:, :, :], iota8[:, :, :], ALU.mult).then_inc(v_leq, 1)
                wait(dve, v_leq, g.times(2, 2))
                dve.tensor_reduce(first[:, :], leq[:, :, :], AX_X, ALU.min).then_inc(v_first, 1)
                wait(dve, v_first, g.times(1, 1))
                dve.tensor_tensor(oh[:, :, :], iota8[:, :, :], spread(first), ALU.is_equal).then_inc(v_oh, 1)
                wait(dve, a_ex, g.times(1, 1))
                dve.tensor_reduce(se[:, :], ex[:, :, :], AX_X, ALU.add).then_inc(v_se, 1)
                wait(dve, v_se, g.times(1, 1))
                dve.reciprocal(h[:, bass.ds(g.times(GB), GB), D], se[:, :]).then_inc(v_w, 1)

            def place(g):
                wait(dve, pe_rk, g.times(1, 1))
                wait(dve, v_base, g.times(1, 1))
                rk = bM2[:, 0:GB * E].rearrange("p (b e) -> p b e", b=GB)
                dve.tensor_tensor(cn[:, :, :], rk, base[:, :].unsqueeze(1).to_broadcast([P, GB, E]), ALU.add
                                  ).then_inc(v_cn, 1)
                wait(dve, v_cn, g.times(1, 1))
                dve.tensor_tensor(base[:, :], bM2[:, GB * E:(GB + 1) * E], base[:, :], ALU.add).then_inc(v_base, 1)
                dve.tensor_tensor(over[:, :, :], cn[:, :, :], limit[:, :].unsqueeze(1).to_broadcast([P, GB, E]),
                                  ALU.is_gt).then_inc(v_over, 1)
                wait(dve, v_over, g.times(1, 1))
                dve.scalar_tensor_tensor(out=pl[:, :, :], in0=over[:, :, :], scalar=BIG, in1=cn[:, :, :],
                                         op0=ALU.mult, op1=ALU.add).then_inc(v_pl, 1)
                wait(dve, v_pl, g.times(1, 1))
                dve.tensor_tensor(pm[:, :, :], pl[:, :, :], oh[:, :, :], ALU.mult).then_inc(v_pm, 1)
                wait(dve, v_pm, g.times(1, 1))
                wait(dve, d_tab, g.times(16 * GB))
                dve.tensor_copy(tid[:, :], tid_all[:, bass.ds(g.times(GB), GB)]).then_inc(v_tid, 1)
                with nc.allow_low_precision(reason="slot numbers are whole and far below 2**24"):
                    dve.tensor_reduce(pos[:, :], pm[:, :, :], AX_X, ALU.add).then_inc(v_pos, 1)

            steps(dve, step)


def expert_phase(nc, sb_in, sem, v):
    b2 = v["b2"]
    D, E, KC, F, FC, SL, NT, TS, NH, N = (v[n] for n in ("D", "E", "KC", "F", "FC", "SL", "NT", "TS", "NH", "N"))
    tab, rows, outf = v["tab"], v["rows"], v["outf"]
    bS, bC, bPV, bM0, bM1, bM2 = (v[n] for n in ("bS", "bC", "bPV", "bM0", "bM1", "bM2"))
    identf, b1t, halfneg, raw, d_raw, load_experts = (
        v[n] for n in ("identf", "b1t", "halfneg", "raw", "d_raw", "load_experts"))
    up_bank = [bS[0], bS[1], bC[0], bC[1]]
    down_bank = [bPV, bM2]
    turn_bank = [bM0, bM1]
    NU = 2 * FC
    TURNS = NT // 2
    PIECES = 8
    PC = 2 * KC * F // PIECES
    STATS_AT = 4
    assert KC * F == FC * D and TURNS % 2 == 1

    with ExitStack() as scope:
        sb = sb_in(scope)
        b2s = sb("b2s", [TS, E, D], F32)
        idx = sb("idx", [TS, E, NT], U32)
        idx_in = sb("idx_in", [TS, NT], U32)
        idx_out = sb("idx_out", [TS, NT], U32)
        xs = [sb(f"xs{q}", [TS, NT, ROW], F32) for q in range(2)]
        st = sb("st", [TS, NT, 6], F32)
        mv = sb("mv", [TS, NT, 2], F32)
        ve = sb("ve", [TS, NT], F32)
        rs = sb("rs", [TS, NT], F32)
        xn = sb("xne", [TS, NT, D], F32)
        xh = [sb(f"xh{q}", [P, KC, SL], F32R) for q in range(2)]
        xl = [sb(f"xl{q}", [P, KC, SL], F32R) for q in range(2)]
        wh = [sb(f"weh{q}", [P, 2 * KC * F], F32R) for q in range(2)]
        wl = [sb(f"wel{q}", [P, 2 * KC * F], F32R) for q in range(2)]
        gl = [sb(f"gl{i}", [P, NH], F32) for i in range(4)]
        hh = sb("hh", [P, FC, SL], F32R)
        hl = sb("hl", [P, FC, SL], F32R)
        yb = [sb(f"yb{j}", [TS, D], F32) for j in range(2)]
        ys = [sb(f"ys{j}", [TS, D], F32) for j in range(NT)]

        d_b2, d_idx, v_xs0 = sem("d_b2"), sem("d_idx"), sem("v_xs0")
        d_xs = [sem(f"d_xs{q}") for q in range(2)]
        d_out = [sem(f"d_out{j}") for j in range(NT)]
        e_turn, e_up, e_down = sem("e_turn"), sem("e_up"), sem("e_down")
        a_xh, a_weh, a_gelu, a_hh = sem("a_xh"), sem("a_weh"), sem("a_gelu"), sem("a_hh")
        v_est, v_emv, v_eve, v_exn, v_xl, v_wel, v_hl, v_yb, v_ys = (
            sem("v_" + n) for n in ("est", "emv", "eve", "exn", "xl", "wel", "hl", "yb", "ys"))
        p_ers, p_in, p_out = sem("p_ers"), sem("p_in"), sem("p_out")

        def expert(n, off):
            if isinstance(n, int) and not 0 <= off < E:
                return None
            return Turn(n, off, 2)

        def steps(eng, step):
            step(0, 0)
            step(0, 1)
            with eng.Fori(0, (E - 4) // 2) as n:
                for c in range(2):
                    step(n, 2 + c)
            step(0, E - 2)
            step(0, E - 1)

        block = scope.enter_context(nc.Block())

        @block.sync
        def _(sp):
            sp.dma_start(idx[:, :, :], tab[:, :].rearrange("(e p j) o -> p e (j o)", e=E, j=NT)).then_inc(d_idx, 16)
            sp.dma_start(b2s[:, :, :], b2.unsqueeze(0).to_broadcast([TS, E, D])).then_inc(d_b2, 16)

            def step(n, i):
                e = expert(n, i + 2)
                if e:
                    hold(sp, a_weh, e.back(1).times(PIECES))
                    hold(sp, v_wel, e.back(1).times(PIECES))
                    load_experts(sp, e.times(1), e.slot)

            steps(sp, step)
            for j in range(NT):
                sp.wait_ge(d_out[j], 16 * E)

        @block.gpsimd
        def _(pool):
            def tokens_in(e):
                if not (isinstance(e.n, int) and e.off == 0):
                    last = e.back(1)
                    hold(pool, d_xs[last.slot], last.round(16 * NT, 16 * NT))
                pool.tensor_copy(idx_in[:, :], idx[:, bass.ds(e.times(1), 1), :].rearrange("p a j -> p (a j)")
                                 ).then_inc(p_in, 1)
                hold(pool, p_in, e.times(1, 1))

            def tokens_out(e):
                for j in range(NT):
                    hold(pool, d_out[j], e.times(16))
                pool.tensor_copy(idx_out[:, :], idx[:, bass.ds(e.times(1), 1), :].rearrange("p a j -> p (a j)")
                                 ).then_inc(p_out, 1)
                hold(pool, p_out, e.times(1, 1))

            def fetch(e, j):
                pool.indirect_dma_start(out=xs[e.slot][:, j, :], out_offset=None, in_=rows[:, :],
                                        in_offset=bass.IndirectOffsetOnAxis(ap=idx_in[:, j:j + 1], axis=0),
                                        bounds_check=N - 1, oob_is_err=False).then_inc(d_xs[e.slot], 16)

            def scale_of(e):
                wait(pool, v_eve, e.times(1, 1))
                pool.tensor_tensor(rs[:, :], ve[:, :], halfneg[0:TS, 0:NT], ALU.pow).then_inc(p_ers, 1)

            pool.wait_ge(d_idx, 16)
            pool.wait_ge(v_xs0, 1)
            tokens_in(expert(0, 0))
            for j in range(NT):
                fetch(expert(0, 0), j)
            scale_of(expert(0, 0))
            pool.wait_ge(v_xs0, 2)
            tokens_in(expert(0, 1))
            for j in range(NT):
                fetch(expert(0, 1), j)

            def step(n, i):
                e, e1, e2 = expert(n, i), expert(n, i + 1), expert(n, i + 2)
                if e1:
                    scale_of(e1)
                tokens_out(e)
                if e2:
                    tokens_in(e2)
                for j in range(NT):
                    hold(pool, v_ys, e.times(NT, j + 1))
                    pool.indirect_dma_start(out=outf,
                                            out_offset=bass.IndirectOffsetOnAxis(ap=idx_out[:, j:j + 1], axis=0),
                                            in_=ys[j][:, :], in_offset=None,
                                            bounds_check=N - 1, oob_is_err=False).then_inc(d_out[j], 16)
                    if e2:
                        fetch(e2, j)

            steps(pool, step)

        @block.scalar
        def _(act):
            def split(e, c):
                q = e.slot
                wait(act, d_raw[q], e.round(32, 32))
                wait(act, e_down, e.back(1).times(NT))
                act.activation(wh[q][:, c * PC:(c + 1) * PC], raw[q][:, c * PC:(c + 1) * PC], ACT.Copy
                               ).then_inc(a_weh, 1)

            def turned(e, r):
                wait(act, e_turn, e.times(TURNS, r + 1))
                act.activation(xh[e.slot][:, :, 2 * r * TS:2 * (r + 1) * TS],
                               turn_bank[r % 2][:, 0:KC * 2 * TS].rearrange("p (k t) -> p k t", k=KC), ACT.Copy
                               ).then_inc(a_xh, 1)

            e0 = expert(0, 0)
            for c in range(PIECES):
                split(e0, c)
            for r in range(TURNS):
                turned(e0, r)

            def step(n, i):
                e, e1 = expert(n, i), expert(n, i + 1)

                def rounded(u):
                    half, f = divmod(u, FC)
                    cols = slice(half * NH, (half + 1) * NH)
                    wait(act, e_down, e.back(1).times(NT, (half + 1) * NT // 2))
                    wait(act, a_gelu, e.times(NU, u + 1))
                    act.activation(hh[:, f, cols], gl[u % 4][:, :], ACT.Copy).then_inc(a_hh, 1)

                for u in range(NU):
                    wait(act, e_up, e.times(NU, u + 1))
                    hold(act, v_hl, e.times(NU, u - 3))
                    act.activation(gl[u % 4][:, :], up_bank[u % 4][:, 0:NH], ACT.Gelu,
                                   bias=b1t[:, bass.ds(e.times(FC, u % FC), 1)]).then_inc(a_gelu, 1)
                    if u:
                        rounded(u - 1)
                rounded(NU - 1)
                if e1:
                    for r in range(TURNS):
                        split(e1, 2 * r)
                        split(e1, 2 * r + 1)
                        turned(e1, r)
                    for c in range(2 * TURNS, PIECES):
                        split(e1, c)

            steps(act, step)

        @block.tensor
        def _(pe):
            def turn(e, r):
                wait(pe, v_exn, e.times(NT, 2 * r + 2))
                wait(pe, v_xl, e.times(TURNS, r - 1 if r == 2 else r))
                for k in range(KC):
                    for j in range(2):
                        at = (k * 2 + j) * TS
                        last = pe.transpose(turn_bank[r % 2][:, at:at + TS], xn[:, 2 * r + j, k * P:(k + 1) * P],
                                            identf[0:TS, 0:TS])
                last.then_inc(e_turn, 1)

            for r in range(TURNS):
                turn(expert(0, 0), r)

            def step(n, i):
                e, e1 = expert(n, i), expert(n, i + 1)
                q = e.slot
                w1 = [w[q][:, 0:KC * F].rearrange("p (k f) -> p k f", k=KC) for w in (wh, wl)]
                w2 = [w[q][:, KC * F:].rearrange("p (c d) -> p c d", c=FC) for w in (wh, wl)]
                xt = [xh[q], xl[q]]
                ht = [hh, hl]
                three = ((0, 0), (0, 1), (1, 0))
                for u in range(NU):
                    half, f = divmod(u, FC)
                    wait(pe, v_xl, e.times(TURNS, TURNS))
                    wait(pe, v_wel, e.times(PIECES, PIECES // 2))
                    wait(pe, a_gelu, e.times(NU, u - 3))
                    terms = [(k, a, b) for k in range(KC) for a, b in three]
                    for m, (k, a, b) in enumerate(terms):
                        last = pe.matmul(up_bank[u % 4][:, 0:NH], w1[a][:, k, f * P:(f + 1) * P],
                                         xt[b][:, k, half * NH:(half + 1) * NH],
                                         start=(m == 0), stop=(m == len(terms) - 1))
                    last.then_inc(e_up, 1)
                for j in range(NT):
                    wait(pe, v_hl, e.times(NU, FC * (1 + j // (NT // 2))))
                    wait(pe, v_wel, e.times(PIECES, PIECES))
                    wait(pe, v_yb, e.times(NT, j - 1))
                    terms = [(c, a, b) for c in range(FC) for a, b in three]
                    for m, (c, a, b) in enumerate(terms):
                        last = pe.matmul(down_bank[j % 2][0:TS, 0:D], ht[a][:, c, j * TS:(j + 1) * TS],
                                         w2[b][:, c, :], start=(m == 0), stop=(m == len(terms) - 1))
                    last.then_inc(e_down, 1)
                    if e1 and j < TURNS:
                        turn(e1, j)

            steps(pe, step)

        @block.vector
        def _(dve):
            for q in range(2):
                dve.memset(xs[q][:, :, :], 0.0).then_inc(v_xs0, 1)

            def split(e, c):
                q = e.slot
                wait(dve, a_weh, e.times(PIECES, c + 1))
                dve.tensor_tensor(wl[q][:, c * PC:(c + 1) * PC], raw[q][:, c * PC:(c + 1) * PC],
                                  wh[q][:, c * PC:(c + 1) * PC].bitcast(F32), ALU.subtract).then_inc(v_wel, 1)

            def stats(e, j):
                if j == 0:
                    wait(dve, d_xs[e.slot], e.round(16 * NT, 16 * NT))
                    hold(dve, v_exn, e.times(NT))
                dve.bn_stats(st[:, j, :], xs[e.slot][:, j, 0:D]).then_inc(v_est, 1)

            def aggregate(e):
                hold(dve, v_est, e.times(NT, NT))
                for j in range(NT):
                    last = dve.bn_aggr(mv[:, j, :], st[:, j, :])
                last.then_inc(v_emv, 1)
                wait(dve, v_emv, e.times(1, 1))
                dve.tensor_scalar(ve[:, :], mv[:, :, 1], EPS, None, ALU.add).then_inc(v_eve, 1)

            def normalise(e, j):
                wait(dve, p_ers, e.times(1, 1))
                wait(dve, e_turn, e.times(TURNS))
                dve.tensor_scalar(xn[:, j, :], xs[e.slot][:, j, 0:D], mv[:, j, 0:1], rs[:, j:j + 1],
                                  ALU.subtract, ALU.mult).then_inc(v_exn, 1)

            def turned(e, r):
                wait(dve, a_xh, e.times(TURNS, r + 1))
                at = slice(2 * r * TS, 2 * (r + 1) * TS)
                dve.tensor_tensor(xl[e.slot][:, :, at],
                                  turn_bank[r % 2][:, 0:KC * 2 * TS].rearrange("p (k t) -> p k t", k=KC),
                                  xh[e.slot][:, :, at].bitcast(F32), ALU.subtract).then_inc(v_xl, 1)

            e0 = expert(0, 0)
            for c in range(PIECES):
                split(e0, c)
            for j in range(NT):
                stats(e0, j)
            aggregate(e0)
            for j in range(NT):
                normalise(e0, j)
            for r in range(TURNS):
                turned(e0, r)
            dve.wait_ge(d_b2, 16)

            def step(n, i):
                e, e1 = expert(n, i), expert(n, i + 1)
                for u in range(NU):
                    half, f = divmod(u, FC)
                    cols = slice(half * NH, (half + 1) * NH)
                    wait(dve, a_hh, e.times(NU, u + 1))
                    dve.tensor_tensor(hl[:, f, cols], gl[u % 4][:, :], hh[:, f, cols].bitcast(F32), ALU.subtract
                                      ).then_inc(v_hl, 1)
                    if e1 and STATS_AT <= u < STATS_AT + NT:
                        stats(e1, u - STATS_AT)
                    if e1 and u == STATS_AT + NT:
                        aggregate(e1)
                    if e1 and u >= NU - 3:
                        normalise(e1, 2 * (u - NU + 3))
                        normalise(e1, 2 * (u - NU + 3) + 1)
                if e1:
                    split(e1, 0)
                    split(e1, 1)
                for j in range(NT):
                    wait(dve, e_down, e.times(NT, j + 1))
                    wait(dve, v_ys, e.times(NT, j - 1))
                    dve.tensor_tensor(yb[j % 2][:, :], down_bank[j % 2][0:TS, 0:D],
                                      b2s[:, bass.ds(e.times(1), 1), :].rearrange("p a d -> p (a d)"), ALU.add
                                      ).then_inc(v_yb, 1)
                    wait(dve, v_yb, e.times(NT, j + 1))
                    wait(dve, d_out[j], e.times(16))
                    dve.scalar_tensor_tensor(out=ys[j][:, :], in0=yb[j % 2][:, :],
                                             scalar=xs[e.slot][:, j, D:D + 1], in1=xs[e.slot][:, j, 0:D],
                                             op0=ALU.mult, op1=ALU.add).then_inc(v_ys, 1)
                    if e1 and j < TURNS:
                        turned(e1, j)
                    if e1:
                        for c in ((2,), (3,), (4,), (5, 6), (7,), ())[j]:
                            split(e1, c)

            steps(dve, step)


_INS = ["x", "L0_tok_weight", "L0_attn_q_proj", "L0_attn_k_proj", "L0_attn_v_proj", "L0_attn_o_proj",
        "L0_ffn_wg", "L0_ffn_W1", "L0_ffn_b1", "L0_ffn_W2", "L0_ffn_b2"]


def kernel(**inputs):
    import numpy as _np
    import concourse.bacc as _bacc
    from concourse import mybir as _mybir
    from concourse.bass_utils import run_bass_kernel_spmd as _run

    nc = _bacc.Bacc("TRN2", target_bir_lowering=False, num_devices=1)
    arrays, args = {}, []
    for name in _INS:
        a = _np.ascontiguousarray(inputs[name])
        arrays[f"in_{name}_dram"] = a
        args.append(nc.dram_tensor(f"in_{name}_dram", a.shape, _mybir.dt.from_np(a.dtype), kind="ExternalInput").ap())
    nb, s = inputs["x"].shape
    d = inputs["L0_tok_weight"].shape[1]
    args.append(nc.dram_tensor("out_0_dram", (nb, s, d), _mybir.dt.float32, kind="ExternalOutput").ap())
    lm_block(nc, *args)
    r = _run(nc, [arrays], core_ids=[0])
    return r.results[0]["out_0_dram"]
```

```python
from contextlib import ExitStack

import concourse.bass as bass
from concourse import mybir

P = 128
F32 = mybir.dt.float32
F32R = mybir.dt.float32r
BF16 = mybir.dt.bfloat16
U32 = mybir.dt.uint32
I32 = mybir.dt.int32
ALU = mybir.AluOpType
ACT = mybir.ActivationFunctionType
AX_X = mybir.AxisListType.X

EPS = 1e-5
MASKED = -1e30
RING = 4
UNITS = 8
AHEAD = 6
ROW = 260


class Turn:

    def __init__(self, n, off, period):
        self.n, self.off, self.period = n, off, period
        self.slot = off % period

    def times(self, per, more=0):
        base = per * self.off + more
        return base if isinstance(self.n, int) else self.n * (per * self.period) + base

    def round(self, per, more=0):
        base = per * (self.off // self.period) + more
        return base if isinstance(self.n, int) else self.n * per + base

    def back(self, k):
        return Turn(self.n, self.off - k, self.period)


def wait(engine, semaphore, value):
    if isinstance(value, int) and value <= 0:
        return
    engine.wait_ge(semaphore, value)


def hold(engine, semaphore, value):
    wait(engine, semaphore, value)
    if not isinstance(value, int):
        engine.nop(nofuse=True)


def lm_block(nc, x, table, wq, wk, wv, wo, wg, W1, b1, W2, b2, out):
    NB, S = x.shape
    D = table.shape[1]
    E, _, F = W1.shape
    H, DK = 16, D // 16
    N = NB * S
    CAP = int(N / E * 1.25) + 1
    KC = D // P
    GB = 2
    NG = NB // GB
    GT = GB * S
    QUADS = H // 4
    PARTS = 3
    KS_ROWS = 6 * DK
    SCALE = float(DK) ** -0.5
    NT = 6
    TS = -(-CAP // NT)
    TS += TS % 2
    SL = NT * TS
    NH = SL // 2
    FC = F // P
    NOWHERE = 1 << 20
    assert S == P and TS <= P and NH <= 512

    tab = nc.dram_tensor("token_of_slot", [E * SL, 1], U32)
    rows = nc.dram_tensor("h_rows", [N, ROW], F32)
    qparts = [nc.dram_tensor(f"q_parts{i}", [PARTS, D, GT], BF16) for i in range(RING)]
    kparts = [nc.dram_tensor(f"k_parts{i}", [PARTS, D, GT], BF16) for i in range(RING)]
    outf = out.rearrange("b s d -> (b s) d")

    with ExitStack() as whole:
        def sb_in(scope):
            return lambda name, shape, dt: scope.enter_context(nc.sbuf_tensor(name, shape, dt))

        sb = sb_in(whole)

        def sem(name):
            return whole.enter_context(nc.semaphore(name))

        bank = {n: whole.enter_context(nc.psum_tensor(n, [P, 512], F32))
                for n in ("S0", "S1", "C0", "C1", "PV", "M0", "M1", "M2")}
        bS = [bank["S0"], bank["S1"]]
        bC = [bank["C0"], bank["C1"]]
        bPV, bM0, bM1, bM2 = bank["PV"], bank["M0"], bank["M1"], bank["M2"]

        identf = sb("identf", [P, P], F32)
        raw = [sb(f"w_raw{q}", [P, 2 * KC * F], F32) for q in range(2)]
        b1t = sb("b1t", [P, E * FC], F32)
        halfneg = sb("halfneg", [P, 8], F32)
        d_raw = [sem(f"d_raw{q}") for q in range(2)]

        def load_experts(eng, e, q):
            eng.dma_start(raw[q][:, 0:KC * F].rearrange("p (k f) -> p k f", k=KC),
                          W1[bass.ds(e, 1)].rearrange("a (k p) f -> p (a k) f", p=P)).then_inc(d_raw[q], 16)
            eng.dma_start(raw[q][:, KC * F:].rearrange("p (c d) -> p c d", c=FC),
                          W2[bass.ds(e, 1)].rearrange("a (c p) d -> p (a c) d", p=P)).then_inc(d_raw[q], 16)

        attention_phase(nc, sb_in, sem, locals())
        expert_phase(nc, sb_in, sem, locals())


def attention_phase(nc, sb_in, sem, v):
    x, table, wq, wk, wv, wo, wg, b1 = (v[n] for n in ("x", "table", "wq", "wk", "wv", "wo", "wg", "b1"))
    NB, S, D, E, H, DK, CAP, KC, GB, NG, GT, QUADS = (
        v[n] for n in ("NB", "S", "D", "E", "H", "DK", "CAP", "KC", "GB", "NG", "GT", "QUADS"))
    PARTS, KS_ROWS, SCALE, SL, FC, NOWHERE, N = (
        v[n] for n in ("PARTS", "KS_ROWS", "SCALE", "SL", "FC", "NOWHERE", "N"))
    tab, rows, qparts, kparts, outf = (v[n] for n in ("tab", "rows", "qparts", "kparts", "outf"))
    bS, bC, bPV, bM0, bM1, bM2 = (v[n] for n in ("bS", "bC", "bPV", "bM0", "bM1", "bM2"))
    identf, b1t, halfneg, raw, load_experts = (v[n] for n in ("identf", "b1t", "halfneg", "raw", "load_experts"))
    BIG = float(NOWHERE)

    with ExitStack() as scope:
        sb = sb_in(scope)
        identb = sb("identb", [P, P], BF16)
        maskb = sb("maskb", [P, 4, S], BF16)
        trib = sb("trib", [P, P], BF16)
        onesb = sb("onesb", [P, P], BF16)
        eps_of = sb("eps_of", [P, GB * E], I32)
        iota8 = sb("iota8", [P, GB, E], F32)
        base = sb("base", [P, E], F32)
        limit = sb("limit", [P, E], F32)
        tid_all = sb("tid_all", [P, NB], U32)
        nowhere = sb("nowhere", [96, E * SL // 96], U32)
        wraw = raw[1][:, 0:4 * KC * D].rearrange("p (m c d) -> p m c d", m=4, c=KC)
        wh = [sb(f"wh{m}", [P, KC, D], F32R) for m in range(4)]
        wl = [sb(f"wl{m}", [P, KC, D], F32R) for m in range(4)]
        wgs = sb("wgs", [P, KC, E], F32)
        b1raw = sb("b1raw", [E * FC, P], F32)
        xi = sb("xi", [NB, S], I32)
        xf = sb("xf", [NB, S], F32)
        idt = sb("idt", [P, NB], U32)
        h = sb("h", [P, NB, ROW], F32)
        st1 = sb("st1", [P, GB, 6], F32)
        mv1 = sb("mv1", [P, GB, 2], F32)
        ve1 = sb("ve1", [P, GB], F32)
        rs1 = sb("rs1", [P, GB], F32)
        xn = sb("xn", [P, GB, D], F32)
        xth = sb("xth", [P, KC, GT], F32R)
        xtl = sb("xtl", [P, KC, GT], F32R)
        qp = sb("qp", [P, PARTS, KC, GT], BF16)
        kp = sb("kp", [P, PARTS, KC, GT], BF16)
        qr = sb("qr", [P, KC, GT], F32)
        kr = sb("kr", [P, KC, GT], F32)
        qs = [sb(f"qs{i}", [KS_ROWS + 1, H, GT], BF16) for i in range(RING)]
        ks = [sb(f"ks{i}", [KS_ROWS + 1, H, GT], BF16) for i in range(RING)]
        va = [sb(f"va{i}", [P, GB, H, 2 * DK], F32) for i in range(RING)]
        mx = [sb(f"mx{i}", [P, H, GB], F32) for i in range(RING)]
        nm = [sb(f"nm{i}", [GB * H, S], BF16) for i in range(RING)]
        pt = [sb(f"pt{i}", [P, 4, S], F32) for i in range(4)]
        osb = [sb(f"os{i}", [P, QUADS, S], F32) for i in range(GB)]
        rec = sb("rec", [P, GB, H], F32)
        on = sb("on", [P, GB, D], F32)
        oth = sb("oth", [P, KC, GT], F32R)
        otl = sb("otl", [P, KC, GT], F32R)
        st2 = sb("st2", [P, GB, 6], F32)
        mv2 = sb("mv2", [P, GB, 2], F32)
        ve2 = sb("ve2", [P, GB], F32)
        rs2 = sb("rs2", [P, GB], F32)
        xn2 = sb("xn2", [P, GB, D], F32)
        x2t = sb("x2t", [P, KC, GT], F32)
        lmax = sb("lmax", [P, GB], F32)
        leq = sb("leq", [P, GB, E], F32)
        first = sb("first", [P, GB], F32)
        oh = sb("oh", [P, GB, E], BF16)
        dl = sb("dl", [P, GB, E], F32)
        ex = sb("ex", [P, GB, E], F32)
        se = sb("se", [P, GB], F32)
        cn = sb("cn", [P, GB, E], F32)
        over = sb("over", [P, GB, E], F32)
        pl = sb("pl", [P, GB, E], F32)
        pm = sb("pm", [P, GB, E], F32)
        pos = sb("pos", [P, GB], U32)
        tid = sb("tid", [P, GB], U32)

        d_x, d_w, d_c, d_init, d_ones, v_ones = (sem(n) for n in ("d_x", "d_w", "d_c", "d_init", "d_ones", "v_ones"))
        d_g = [sem(f"d_g{i}") for i in range(RING)]
        d_qw, d_kw = sem("d_qw"), sem("d_kw")
        d_q = [sem(f"d_q{i}") for i in range(RING)]
        d_k = [sem(f"d_k{i}") for i in range(RING)]
        d_sh = [sem(f"d_sh{i}") for i in range(RING)]
        d_rows, d_tab = sem("d_rows"), sem("d_tab")
        g_set, g_cst, v_cst = sem("g_set"), sem("g_cst"), sem("v_cst")
        v_xf, pe_id, v_idt, pe_w, a_wh, v_wl = (sem(n) for n in ("v_xf", "pe_id", "v_idt", "pe_w", "a_wh", "v_wl"))
        pe_b1, v_b1 = sem("pe_b1"), sem("v_b1")
        pe_T, pe_Q, pe_K, pe_V, pe_S, pe_mT, pe_C, pe_PV, pe_OT, pe_oT, pe_O, pe_x2T, pe_lg, pe_rk = (
            sem("pe_" + n) for n in ("T", "Q", "K", "V", "S", "mT", "C", "PV", "OT", "oT", "O", "x2T", "lg", "rk"))
        a_xth, a_q1, a_q2, a_k1, a_k2, a_V, a_exp, a_nm, a_os, a_oth, a_x2t, a_ex = (
            sem("a_" + n) for n in ("xth", "q1", "q2", "k1", "k2", "V", "exp", "nm", "os", "oth", "x2t", "ex"))
        v_st1, v_mv1, v_ve1, v_xn, v_xtl, v_qr, v_kr, v_mx, v_rec, v_on, v_otl = (
            sem("v_" + n) for n in ("st1", "mv1", "ve1", "xn", "xtl", "qr", "kr", "mx", "rec", "on", "otl"))
        v_h1, v_st2, v_mv2, v_ve2, v_xn2, v_lmax, v_leq, v_first, v_dl, v_se, v_w = (
            sem("v_" + n) for n in ("h1", "st2", "mv2", "ve2", "xn2", "lmax", "leq", "first", "dl", "se", "w"))
        v_oh, v_cn, v_over, v_pl, v_pm, v_base, v_tid, v_pos = (
            sem("v_" + n) for n in ("oh", "cn", "over", "pl", "pm", "base", "tid", "pos"))
        p_q3, p_k3, p_sel, p_rs1, p_rs2 = (sem("p_" + n) for n in ("q3", "k3", "sel", "rs1", "rs2"))

        def group(n, off):
            if isinstance(n, int) and not 0 <= off < NG:
                return None
            return Turn(n, off, RING)

        FIRST = AHEAD + 1
        ROUNDS = (NG - 1 - FIRST) // RING
        AFTER = FIRST + RING * ROUNDS
        LAST = NG + AHEAD

        def steps(eng, step):
            for i in range(FIRST):
                step(0, i)
            with eng.Fori(0, ROUNDS) as n:
                for c in range(RING):
                    step(n, FIRST + c)
            for i in range(AFTER, LAST):
                step(0, i)

        def shift_unit(n, i, s, lag):
            d, u = divmod(s - lag, UNITS)
            return group(n, i + d), u

        S_LAG, C_LAG, PV_LAG = UNITS + 4, 2 * UNITS + 7, 3 * UNITS + 1

        def weight_columns(w, m):
            bank = (bM1, bM2, bS[0], bS[1])[m]
            if m > 1:
                return [(w[:, :, :], bank[:, :].rearrange("p (k d) -> p k d", k=KC))]
            return [(w[:, k, c * P:(c + 1) * P].rearrange("p (d j) -> p d j", d=DK),
                     bank[:, k * D:(k + 1) * D].rearrange("p (j c d) -> p c d j", c=KC, d=DK)[:, c])
                    for k in range(KC) for c in range(KC)]

        block = scope.enter_context(nc.Block())

        @block.sync
        def _(sp):
            sp.dma_start(xi[:, :], x).then_inc(d_x, 16)
            for m, w in enumerate((wq, wk, wv, wo)):
                sp.dma_start(wraw[:, m], w.rearrange("(c p) d -> p c d", p=P)).then_inc(d_w, 16)
            sp.dma_start(wgs[:, :, :], wg.rearrange("(k p) e -> p k e", p=P)).then_inc(d_c, 16)
            sp.dma_start(b1raw[:, :], b1.rearrange("e (c p) -> (e c) p", p=P)).then_inc(d_c, 16)
            sp.wait_ge(g_set, 1)
            sp.dma_start(tab[:, :].rearrange("(p n) o -> p (n o)", p=96), nowhere[:, :]).then_inc(d_init, 16)
            sp.wait_ge(v_ones, 1)
            for i in range(RING):
                sp.dma_start(ks[i][KS_ROWS:KS_ROWS + 1, :, :], onesb[0:H * GT // P, :]).then_inc(d_ones, 16)
            load_experts(sp, 0, 0)
            sp.wait_ge(pe_w, 4)
            load_experts(sp, 1, 1)

            def stacks_q(parts, stacked, done):
                at = 0
                for part, times in enumerate((3, 2, 1)):
                    sp.dma_start(stacked[at:at + times * DK, :, :],
                                 parts[part].rearrange("(d h) t -> d h t", d=DK).unsqueeze(0)
                                 .to_broadcast([times, DK, H, GT])).then_inc(done, 16)
                    at += times * DK

            def stacks_k(parts, stacked, done):
                at = 0
                for count in (3, 2, 1):
                    sp.dma_start(stacked[at:at + count * DK, :, :],
                                 parts[0:count].rearrange("a (d h) t -> (a d) h t", d=DK)).then_inc(done, 16)
                    at += count * DK

            def step(n, i):
                g = group(n, i)
                if g:
                    hold(sp, pe_C, g.back(RING - 1).times(UNITS))
                    hold(sp, p_q3, g.times(1, 1))
                    sp.dma_start(qparts[g.slot][:, :, :].rearrange("a (p k) t -> p a (k t)", p=P),
                                 qp[:, :, :, :].rearrange("p a k t -> p a (k t)")).then_inc(d_qw, 16)
                    hold(sp, p_k3, g.times(1, 1))
                    sp.dma_start(kparts[g.slot][:, :, :].rearrange("a (p k) t -> p a (k t)", p=P),
                                 kp[:, :, :, :].rearrange("p a k t -> p a (k t)")).then_inc(d_kw, 16)
                g2 = group(n, i - 2)
                if g2:
                    hold(sp, a_nm, g2.times(1, 1))
                    hold(sp, pe_C, g2.back(RING - 1).times(UNITS))
                    sp.dma_start(qs[g2.slot][KS_ROWS:KS_ROWS + 1, :, :].rearrange("p h (b t) -> p (h b) t", b=GB),
                                 nm[g2.slot][:, :]).then_inc(d_sh[g2.slot], 16)
                if g:
                    hold(sp, d_qw, g.times(16, 16))
                    stacks_q(qparts[g.slot], qs[g.slot], d_q[g.slot])
                    hold(sp, d_kw, g.times(16, 16))
                    stacks_k(kparts[g.slot], ks[g.slot], d_k[g.slot])
                g = group(n, i - 6)
                if g:
                    hold(sp, v_w, g.times(1, 1))
                    hg = h[:, bass.ds(g.times(GB), GB), :]
                    sp.dma_start(rows[bass.ds(g.times(GT), GT), :].rearrange("(b p) c -> p b c", p=P),
                                 hg).then_inc(d_rows, 16)
                    sp.dma_start(outf[bass.ds(g.times(GT), GT), :].rearrange("(b p) c -> p b c", p=P),
                                 hg[:, :, 0:D]).then_inc(d_rows, 16)

            steps(sp, step)
            sp.wait_ge(d_rows, 32 * NG)
            sp.wait_ge(d_tab, 32 * NG)

        @block.gpsimd
        def _(pool):
            pool.memset(identf[:, :], 0.0).then_inc(g_cst, 1)
            pool.memset(nowhere[:, :], NOWHERE).then_inc(g_set, 1)
            pool.memset(maskb[:, :, :], 0.0).then_inc(g_cst, 1)
            pool.memset(trib[:, :], 1.0).then_inc(g_cst, 1)
            pool.wait_ge(g_cst, 3)
            pool.affine_select(out=identf[:, :], in_=identf[:, :], compare_op=ALU.not_equal, fill=1.0, base=0,
                               pattern=[[-1, P]], channel_multiplier=1).then_inc(g_set, 1)
            pool.affine_select(out=maskb[:, :, :], in_=maskb[:, :, :], compare_op=ALU.is_ge, fill=MASKED, base=0,
                               pattern=[[0, 4], [-1, S]], channel_multiplier=1).then_inc(g_set, 1)
            pool.affine_select(out=trib[:, :], in_=trib[:, :], compare_op=ALU.is_ge, fill=0.0, base=0,
                               pattern=[[1, P]], channel_multiplier=-1).then_inc(g_set, 1)
            pool.iota(eps_of[:, :], pattern=[[0, GB], [1, E]], base=0, channel_multiplier=0).then_inc(g_set, 1)
            pool.iota(tid_all[:, :], pattern=[[P, NB]], base=0, channel_multiplier=1).then_inc(g_set, 1)

            def store_slots(g, b):
                hold(pool, v_tid, g.times(1, 1))
                hold(pool, v_pos, g.times(1, 1))
                pool.indirect_dma_start(out=tab[:, :],
                                        out_offset=bass.IndirectOffsetOnAxis(ap=pos[:, b:b + 1], axis=0),
                                        in_=tid[:, b:b + 1], in_offset=None,
                                        bounds_check=E * SL - 1, oob_is_err=False).then_inc(d_tab, 16)

            def gather(g):
                wait(pool, d_g[g % RING], 16 * GB * (g // RING))
                for b in range(GB * g, GB * g + GB):
                    pool.indirect_dma_start(out=h[:, b, 0:D], out_offset=None, in_=table,
                                            in_offset=bass.IndirectOffsetOnAxis(ap=idt[:, b:b + 1], axis=0)
                                            ).then_inc(d_g[g % RING], 16)

            gathers = list(range(NG))
            pool.wait_ge(v_idt, 1)
            for g in gathers[:2]:
                gather(g)
            del gathers[:2]
            pool.wait_ge(v_cst, 3)
            pool.wait_ge(v_ve1, 1)
            pool.tensor_tensor(rs1[:, :], ve1[:, :], halfneg[:, 0:GB], ALU.pow).then_inc(p_rs1, 1)
            for g in gathers[:1]:
                gather(g)
            del gathers[:1]

            pool.wait_ge(d_init, 16)

            def step(n, i):
                for s in range(UNITS):
                    g, u = shift_unit(n, i, s, C_LAG)
                    if g:
                        buf = pt[u % 4]
                        hold(pool, a_exp, g.times(UNITS, u + 1))
                        pool.affine_select(out=buf[:, :, :], in_=buf[:, :, :], compare_op=ALU.is_ge, fill=0.0,
                                           base=0, pattern=[[0, 4], [1, S]], channel_multiplier=-1
                                           ).then_inc(p_sel, 1)
                    g = group(n, i)
                    if g and s == 2:
                        wait(pool, a_q2, g.times(1, 1))
                        pool.tensor_tensor(qp[:, 2], qr[:, :, :], qp[:, 1], ALU.subtract).then_inc(p_q3, 1)
                    if g and s == 3:
                        wait(pool, a_k2, g.times(1, 1))
                        pool.tensor_tensor(kp[:, 2], kr[:, :, :], kp[:, 1], ALU.subtract).then_inc(p_k3, 1)
                    g = group(n, i + 1)
                    if g and s == 5:
                        wait(pool, v_ve1, g.times(1, 1))
                        pool.tensor_tensor(rs1[:, :], ve1[:, :], halfneg[:, 0:GB], ALU.pow).then_inc(p_rs1, 1)
                    g = group(n, i - 4)
                    if g and s == 7:
                        wait(pool, v_ve2, g.times(1, 1))
                        pool.tensor_tensor(rs2[:, :], ve2[:, :], halfneg[:, 0:GB], ALU.pow).then_inc(p_rs2, 1)
                    g = group(n, i - 6)
                    if g and s in (4, 6):
                        store_slots(g, s // 5)
                    if isinstance(n, int) and gathers and s in (1, 4, 6):
                        gather(gathers.pop(0))
            steps(pool, step)

        @block.scalar
        def _(act):
            for m in range(4):
                act.wait_ge(pe_w, m + 1)
                for dst, src in weight_columns(wh[m], m):
                    last = act.activation(dst, src, ACT.Copy)
                last.then_inc(a_wh, 1)

            def step(n, i):
                def scores(s):
                    g, u = shift_unit(n, i, s, C_LAG)
                    if g:
                        wait(act, pe_C, g.times(UNITS, u + 1))
                        wait(act, pe_PV, g.times(UNITS, u - 3))
                        act.activation(pt[u % 4][:, :, :], bC[u % 2][:, :].rearrange("p (j t) -> p j t", j=4),
                                       ACT.Exp, scale=SCALE).then_inc(a_exp, 1)

                def values(g, b):
                    if g:
                        wait(act, pe_PV, g.times(UNITS, 4 * b + 4))
                        act.activation(osb[b][:, :, :], bPV[:, :].rearrange("p (a t) -> p a t", a=QUADS),
                                       ACT.Copy).then_inc(a_os, 1)

                def first_part(g, done, src, parts, w_done, first_done):
                    wait(act, done, g.times(1, 1))
                    wait(act, w_done, g.times(16))
                    act.activation(parts[:, 0], src[:, :].rearrange("p (k t) -> p k t", k=KC), ACT.Copy
                                   ).then_inc(first_done, 1)

                def second_part(g, rest_done, parts, rest, second_done):
                    wait(act, rest_done, g.times(1, 1))
                    act.activation(parts[:, 1], rest[:, :, :], ACT.Copy).then_inc(second_done, 1)

                def from_bank(dst, src, done, g, signal):
                    wait(act, done, g.times(1, 1))
                    act.activation(dst[:, :, :], src[:, :].rearrange("p (k t) -> p k t", k=KC), ACT.Copy
                                   ).then_inc(signal, 1)

                g0, g2, g3, g4, g5, g6 = (group(n, i - k) for k in (0, 2, 3, 4, 5, 6))
                if g0:
                    from_bank(xth, bM0, pe_T, g0, a_xth)
                scores(0)
                if g6:
                    wait(act, v_dl, g6.times(1, 1))
                    act.activation(ex[:, :, :], dl[:, :, :], ACT.Exp).then_inc(a_ex, 1)
                values(g4, 1)
                scores(1)
                if g0:
                    first_part(g0, pe_Q, bM0, qp, d_qw, a_q1)
                scores(2)
                if g0:
                    second_part(g0, v_qr, qp, qr, a_q2)
                if g0:
                    first_part(g0, pe_K, bM2, kp, d_kw, a_k1)
                scores(3)
                if g4:
                    from_bank(oth, bM1, pe_oT, g4, a_oth)
                if g0:
                    second_part(g0, v_kr, kp, kr, a_k2)
                scores(4)
                if g2:
                    wait(act, pe_mT, g2.times(1, 1))
                    act.activation(nm[g2.slot][:, :], bM2[0:GB * H, 0:S], ACT.Copy, scale=-1.0).then_inc(a_nm, 1)
                values(g3, 0)
                scores(5)
                if g5:
                    from_bank(x2t, bM2, pe_x2T, g5, a_x2t)
                scores(6)
                scores(7)
                if g0:
                    wait(act, pe_V, g0.times(1, 1))
                    wait(act, pe_PV, g0.back(RING - 1).times(UNITS))
                    act.activation(va[g0.slot][:, :, :, 0:DK].rearrange("p b h d -> p (b h) d"),
                                   bM1[:, :].rearrange("p (c d) -> p c d", d=DK), ACT.Copy).then_inc(a_V, 1)

            steps(act, step)

        @block.tensor
        def _(pe):
            pe.wait_ge(g_set, 2)
            pe.wait_ge(v_xf, 1)
            pe.transpose(bM0[:, 0:NB], xf[:, :], identf[0:NB, 0:NB]).then_inc(pe_id, 1)
            pe.wait_ge(d_w, 64)
            for m in range(4):
                dst = [bM1, bM2, bS[0], bS[1]][m]
                for k in range(KC):
                    for c in range(KC):
                        last = pe.transpose(dst[:, k * D + c * P:k * D + (c + 1) * P],
                                            wraw[:, m, c, k * P:(k + 1) * P], identf[:, :])
                last.then_inc(pe_w, 1)
            pe.wait_ge(d_c, 32)
            pe.transpose(bC[0][:, 0:E * FC], b1raw[:, :], identf[0:E * FC, 0:E * FC]).then_inc(pe_b1, 1)
            pe.wait_ge(a_wh, 4)
            pe.wait_ge(v_wl, 4)
            pe.wait_ge(v_idt, 1)
            pe.wait_ge(v_b1, 1)
            pe.wait_ge(v_cst, 6)
            pe.wait_ge(v_ones, 1)
            pe.wait_ge(d_ones, 16 * RING)
            pe.wait_ge(g_set, 6)

            def passes(dst, lhs, rhs, last_of=None):
                pairs = [(a, b) for k in range(KC) for a, b in ((0, 0), (0, 1), (1, 0))]
                for m, (a, b) in enumerate(pairs):
                    k = m // 3
                    last = pe.matmul(dst, lhs[a](k), rhs[b](k), start=(m == 0), stop=(m == len(pairs) - 1))
                return last

            def turn4(dst, src):
                for k in range(KC):
                    for b in range(GB):
                        at = (k * GB + b) * P
                        last = pe.transpose(dst[:, at:at + P], src[:, b, k * P:(k + 1) * P], identf[:, :])
                return last

            def project(dst, m):
                for c in range(KC):
                    last = passes(dst[:, c * GT:(c + 1) * GT],
                                  [lambda k, w=w, c=c: w[m][:, k, c * P:(c + 1) * P] for w in (wh, wl)],
                                  [lambda k, t=t: t[:, k, :] for t in (xth, xtl)])
                return last

            def turn_values(dst, g, b):
                wait(pe, a_os, g.times(GB, b + 1))
                for a in range(QUADS):
                    last = pe.transpose(dst[:, a * P:(a + 1) * P], osb[b][:, a, :], identf[:, :])
                last.then_inc(pe_OT, 1)

            pe.wait_ge(v_xn, 1)
            turn4(bM0, xn).then_inc(pe_T, 1)

            def step(n, i):
                for s in range(UNITS):
                    g, u = shift_unit(n, i, s, S_LAG)
                    if g:
                        if u == 0:
                            wait(pe, d_q[g.slot], g.round(48, 48))
                            wait(pe, d_k[g.slot], g.round(48, 48))
                        dst, b = bS[u % 2], u // QUADS
                        wait(pe, v_mx, g.times(UNITS, u - 1))
                        pe.matmul(dst[:, :], identb[:, :], maskb[:, :, :], start=True, stop=False)
                        for j in range(4):
                            hh = (u % QUADS) * 4 + j
                            last = pe.matmul(dst[:, j * S:(j + 1) * S],
                                             qs[g.slot][0:KS_ROWS, hh, b * S:(b + 1) * S],
                                             ks[g.slot][0:KS_ROWS, hh, b * S:(b + 1) * S],
                                             start=False, stop=(j == 3))
                        last.then_inc(pe_S, 1)
                    g, u = shift_unit(n, i, s, C_LAG)
                    if g:
                        if u == 0:
                            wait(pe, d_sh[g.slot], g.round(16, 16))
                        b = u // QUADS
                        wait(pe, a_exp, g.times(UNITS, u - 1))
                        for j in range(4):
                            hh = (u % QUADS) * 4 + j
                            last = pe.matmul(bC[u % 2][:, j * S:(j + 1) * S],
                                             ks[g.slot][:, hh, b * S:(b + 1) * S],
                                             qs[g.slot][:, hh, b * S:(b + 1) * S], start=True, stop=True)
                        last.then_inc(pe_C, 1)
                    g = group(n, i - 4)
                    if g and s == 2:
                        wait(pe, v_h1, g.times(1))
                        wait(pe, a_V, g.times(1, 4) if group(n, i - 1) else NG)
                        turn_values(bM1, g, 1)
                    if g and s == 3:
                        wait(pe, v_on, g.times(GB, GB))
                        turn4(bM1, on).then_inc(pe_oT, 1)
                    g = group(n, i)
                    if g and s == 2:
                        wait(pe, a_nm, g.back(3).times(1, 1))
                        wait(pe, v_base, g.back(6).times(1, 2))
                        project(bM2, 1).then_inc(pe_K, 1)
                    if g and s == 7:
                        wait(pe, v_h1, g.back(4).times(1, 1))
                        wait(pe, a_V, g.times(1))
                        for b in range(GB):
                            last = passes(bM1[:, b * D:(b + 1) * D],
                                          [lambda k, t=t, b=b: t[:, k, b * S:(b + 1) * S] for t in (xth, xtl)],
                                          [lambda k, w=w: w[2][:, k, :] for w in (wh, wl)])
                        last.then_inc(pe_V, 1)
                    g = group(n, i + 1)
                    if g and s == 7:
                        wait(pe, v_xn, g.times(1, 1))
                        wait(pe, v_qr, g.times(1))
                        wait(pe, v_on, g.back(4).times(GB, 1))
                        turn4(bM0, xn).then_inc(pe_T, 1)
                    g = group(n, i - 2)
                    if g and s == 4:
                        wait(pe, v_mx, g.times(UNITS, UNITS))
                        wait(pe, a_k1, g.times(1, 3) if group(n, i) else NG)
                        wait(pe, v_kr, g.times(1, 3) if group(n, i) else NG)
                        wait(pe, v_base, g.back(4).times(1, 2))
                        pe.transpose(bM2[0:GB * H, 0:S], mx[g.slot][:, :, :].rearrange("p h b -> p (h b)"), identf[:, :]).then_inc(pe_mT, 1)
                    g = group(n, i - 4)
                    if g and s == 5:
                        wait(pe, a_oth, g.times(1, 1))
                        wait(pe, v_otl, g.times(1, 1))
                        for b in range(GB):
                            last = passes(bM1[:, b * D:(b + 1) * D],
                                          [lambda k, t=t, b=b: t[:, k, b * S:(b + 1) * S] for t in (oth, otl)],
                                          [lambda k, w=w: w[3][:, k, :] for w in (wh, wl)])
                        last.then_inc(pe_O, 1)
                    g = group(n, i - 5)
                    if g and s == 5:
                        wait(pe, v_xn2, g.times(1, 1))
                        wait(pe, v_base, g.times(1, 1))
                        wait(pe, a_nm, g.times(1, 4) if group(n, i - 2) else NG)
                        turn4(bM2, xn2).then_inc(pe_x2T, 1)
                    if g and s == 6:
                        wait(pe, a_x2t, g.times(1, 1))
                        for b in range(GB):
                            for k in range(KC):
                                last = pe.matmul(bM2[:, b * E:(b + 1) * E], x2t[:, k, b * S:(b + 1) * S],
                                                 wgs[:, k, :], start=(k == 0), stop=(k == KC - 1))
                        last.then_inc(pe_lg, 1)
                    g = group(n, i - 6)
                    if g and s == 0:
                        wait(pe, v_oh, g.times(1, 1))
                        wait(pe, v_dl, g.times(1, 1))
                        pe.matmul(bM2[:, 0:E], trib[:, :], oh[:, 0, :], start=True, stop=True)
                        pe.matmul(bM2[:, E:2 * E], trib[:, :], oh[:, 1, :], start=True, stop=False)
                        pe.matmul(bM2[:, E:2 * E], onesb[:, :], oh[:, 0, :], start=False, stop=True)
                        pe.matmul(bM2[:, 2 * E:3 * E], onesb[:, :], oh[:, 0, :], start=True, stop=False)
                        pe.matmul(bM2[:, 2 * E:3 * E], onesb[:, :], oh[:, 1, :], start=False, stop=True
                                  ).then_inc(pe_rk, 1)
                    g = group(n, i)
                    if g and s == 1:
                        wait(pe, a_xth, g.times(1, 1))
                        wait(pe, v_xtl, g.times(1, 1))
                        project(bM0, 0).then_inc(pe_Q, 1)
                    g = group(n, i - 3)
                    if g and s == 6:
                        wait(pe, a_q1, g.times(1, 4) if group(n, i) else NG)
                        wait(pe, v_qr, g.times(1, 4) if group(n, i) else NG)
                        wait(pe, v_on, g.times(GB, -1))
                        turn_values(bM0, g, 0)
                    g, u = shift_unit(n, i, s, PV_LAG)
                    if g:
                        b = u // QUADS
                        if u == 0:
                            wait(pe, a_V, g.times(1, 1))
                        if u % QUADS == 0:
                            wait(pe, a_os, g.times(GB, b))
                        wait(pe, p_sel, g.times(UNITS, u + 1))
                        for j in range(4):
                            hh = (u % QUADS) * 4 + j
                            last = pe.matmul(bPV[32 * j:32 * j + 32, (u % QUADS) * S:(u % QUADS + 1) * S],
                                             va[g.slot][:, b, hh, :], pt[u % 4][:, j, :], start=True, stop=True)
                        last.then_inc(pe_PV, 1)

            steps(pe, step)

        @block.vector
        def _(dve):
            dve.wait_ge(d_x, 16)
            dve.tensor_copy(xf[:, :], xi[:, :]).then_inc(v_xf, 1)
            dve.memset(halfneg[:, :], -0.5).then_inc(v_cst, 1)
            dve.memset(onesb[:, :], 1.0).then_inc(v_ones, 1)
            dve.memset(h[:, :, D:ROW], 0.0).then_inc(v_cst, 1)
            dve.wait_ge(g_set, 2)
            dve.tensor_copy(identb[:, :], identf[:, :]).then_inc(v_cst, 1)
            dve.wait_ge(pe_id, 1)
            dve.tensor_copy(idt[:, :], bM0[:, 0:NB]).then_inc(v_idt, 1)
            for i in range(RING):
                last = dve.memset(va[i][:, :, :, DK:2 * DK], 1.0)
            last.then_inc(v_cst, 1)
            dve.wait_ge(g_set, 6)
            dve.tensor_scalar(iota8[:, :, :], eps_of[:, :].rearrange("p (b e) -> p b e", b=GB), -float(E), None,
                              ALU.add).then_inc(v_cst, 1)
            dve.tensor_scalar(base[:, :], eps_of[:, 0:E], float(SL), -1.0, ALU.mult, ALU.add).then_inc(v_base, 1)
            dve.tensor_scalar(limit[:, :], eps_of[:, 0:E], float(SL), float(CAP - 1), ALU.mult, ALU.add
                              ).then_inc(v_cst, 1)
            for m in range(4):
                dve.wait_ge(a_wh, m + 1)
                for (dst, src), (high, _) in zip(weight_columns(wl[m], m), weight_columns(wh[m], m)):
                    last = dve.tensor_tensor(dst, src, high.bitcast(F32), ALU.subtract)
                last.then_inc(v_wl, 1)
            dve.wait_ge(pe_b1, 1)
            dve.tensor_copy(b1t[:, :], bC[0][:, 0:E * FC]).then_inc(v_b1, 1)
            dve.wait_ge(v_cst, 6)

            def stats(g, st, mv, ve, s_st, s_mv, s_ve):
                for b in range(GB):
                    last = dve.bn_stats(st[:, b, :], h[:, bass.ds(g.times(GB, b), 1), 0:D].rearrange("p a d -> p (a d)"))
                last.then_inc(s_st, 1)
                hold(dve, s_st, g.times(1, 1))
                for b in range(GB):
                    last = dve.bn_aggr(mv[:, b, :], st[:, b, :])
                last.then_inc(s_mv, 1)
                wait(dve, s_mv, g.times(1, 1))
                dve.tensor_scalar(ve[:, :], mv[:, :, 1], EPS, None, ALU.add).then_inc(s_ve, 1)

            def normalise(g, dst, mv, rs, done):
                for b in range(GB):
                    last = dve.tensor_scalar(dst[:, b, :],
                                             h[:, bass.ds(g.times(GB, b), 1), 0:D].rearrange("p a d -> p (a d)"),
                                             mv[:, b, 0:1], rs[:, b:b + 1], ALU.subtract, ALU.mult)
                last.then_inc(done, 1)

            def stats1(g):
                wait(dve, d_g[g.slot], g.round(16 * GB, 16 * GB))
                hold(dve, v_xn, g.times(1))
                stats(g, st1, mv1, ve1, v_st1, v_mv1, v_ve1)

            def norm1(g):
                wait(dve, p_rs1, g.times(1, 1))
                normalise(g, xn, mv1, rs1, v_xn)

            g0 = group(0, 0)
            stats1(g0)
            norm1(g0)

            def step(n, i):
                def maxima(s):
                    g, u = shift_unit(n, i, s, S_LAG)
                    if g:
                        wait(dve, pe_S, g.times(UNITS, u + 1))
                        dve.tensor_reduce(mx[g.slot][:, 4 * (u % QUADS):4 * (u % QUADS) + 4, u // QUADS],
                                          bS[u % 2][:, :].rearrange("p (j t) -> p j t", j=4), AX_X, ALU.max
                                          ).then_inc(v_mx, 1)

                def low_part(g, dst, src, high, high_done, signal):
                    wait(dve, high_done, g.times(1, 1))
                    dve.tensor_tensor(dst[:, :, :], src[:, :].rearrange("p (k t) -> p k t", k=KC),
                                      high[:, :, :].bitcast(F32), ALU.subtract).then_inc(signal, 1)

                def rest_of(g, src, parts, rest, first_done, third_done, rest_done):
                    wait(dve, first_done, g.times(1, 1))
                    wait(dve, third_done, g.times(1))
                    dve.tensor_tensor(rest[:, :, :], src[:, :].rearrange("p (k t) -> p k t", k=KC), parts[:, 0],
                                      ALU.subtract).then_inc(rest_done, 1)

                def divide(g, b, bank):
                    src = bank[:, :].rearrange("p (h c) -> p h c", h=H)
                    wait(dve, pe_OT, g.times(GB, b + 1))
                    dve.reciprocal(rec[:, b, :], src[:, :, DK]).then_inc(v_rec, 1)
                    wait(dve, v_rec, g.times(GB, b + 1))
                    dve.tensor_tensor(on[:, b, :].rearrange("p (h d) -> p h d", h=H), src[:, :, 0:DK],
                                      rec[:, b, :].unsqueeze(2).to_broadcast([P, H, DK]), ALU.mult
                                      ).then_inc(v_on, 1)

                g0, g3, g4, g5, g6, nxt = (group(n, i - k) for k in (0, 3, 4, 5, 6, -1))
                if g0:
                    low_part(g0, xtl, bM0, xth, a_xth, v_xtl)
                maxima(0)
                if g6:
                    weigh(g6)
                maxima(1)
                if g6:
                    place(g6)
                if g0:
                    rest_of(g0, bM0, qp, qr, a_q1, p_q3, v_qr)
                maxima(2)
                if g4:
                    divide(g4, 1, bM1)
                if g0:
                    rest_of(g0, bM2, kp, kr, a_k1, p_k3, v_kr)
                maxima(3)
                if g4:
                    low_part(g4, otl, bM1, oth, a_oth, v_otl)
                if g5:
                    wait(dve, p_rs2, g5.times(1, 1))
                    normalise(g5, xn2, mv2, rs2, v_xn2)
                maxima(4)
                if nxt:
                    stats1(nxt)
                maxima(5)
                if g4:
                    wait(dve, pe_O, g4.times(1, 1))
                    hg = h[:, bass.ds(g4.times(GB), GB), 0:D]
                    dve.tensor_tensor(hg, bM1[:, :].rearrange("p (b d) -> p b d", b=GB), hg, ALU.add
                                      ).then_inc(v_h1, 1)
                if nxt:
                    norm1(nxt)
                maxima(6)
                if g3:
                    divide(g3, 0, bM0)
                if g4:
                    wait(dve, v_h1, g4.times(1, 1))
                    hold(dve, v_xn2, g4.times(1))
                    stats(g4, st2, mv2, ve2, v_st2, v_mv2, v_ve2)
                maxima(7)
                if g5:
                    route(g5)

            def spread(t):
                return t[:, :].unsqueeze(2).to_broadcast([P, GB, E])

            def route(g):
                lg = bM2[:, 0:GB * E].rearrange("p (b e) -> p b e", b=GB)
                wait(dve, pe_lg, g.times(1, 1))
                dve.tensor_reduce(lmax[:, :], lg, AX_X, ALU.max).then_inc(v_lmax, 1)
                wait(dve, v_lmax, g.times(1, 1))
                dve.tensor_tensor(leq[:, :, :], lg, spread(lmax), ALU.is_equal).then_inc(v_leq, 1)
                dve.tensor_tensor(dl[:, :, :], lg, spread(lmax), ALU.subtract).then_inc(v_dl, 1)
                wait(dve, v_leq, g.times(2, 1))
                dve.tensor_tensor(leq[:, :, :], leq[:, :, :], iota8[:, :, :], ALU.mult).then_inc(v_leq, 1)
                wait(dve, v_leq, g.times(2, 2))
                dve.tensor_reduce(first[:, :], leq[:, :, :], AX_X, ALU.min).then_inc(v_first, 1)
                wait(dve, v_first, g.times(1, 1))
                dve.tensor_tensor(oh[:, :, :], iota8[:, :, :], spread(first), ALU.is_equal).then_inc(v_oh, 1)

            def weigh(g):
                wait(dve, a_ex, g.times(1, 1))
                dve.tensor_reduce(se[:, :], ex[:, :, :], AX_X, ALU.add).then_inc(v_se, 1)
                wait(dve, v_se, g.times(1, 1))
                dve.reciprocal(h[:, bass.ds(g.times(GB), GB), D], se[:, :]).then_inc(v_w, 1)

            def place(g):
                wait(dve, pe_rk, g.times(1, 1))
                wait(dve, v_base, g.times(1, 1))
                rk = bM2[:, 0:GB * E].rearrange("p (b e) -> p b e", b=GB)
                dve.tensor_tensor(cn[:, :, :], rk, base[:, :].unsqueeze(1).to_broadcast([P, GB, E]), ALU.add
                                  ).then_inc(v_cn, 1)
                wait(dve, v_cn, g.times(1, 1))
                dve.tensor_tensor(base[:, :], bM2[:, GB * E:(GB + 1) * E], base[:, :], ALU.add).then_inc(v_base, 1)
                dve.tensor_tensor(over[:, :, :], cn[:, :, :], limit[:, :].unsqueeze(1).to_broadcast([P, GB, E]),
                                  ALU.is_gt).then_inc(v_over, 1)
                wait(dve, v_over, g.times(1, 1))
                dve.scalar_tensor_tensor(out=pl[:, :, :], in0=over[:, :, :], scalar=BIG, in1=cn[:, :, :],
                                         op0=ALU.mult, op1=ALU.add).then_inc(v_pl, 1)
                wait(dve, v_pl, g.times(1, 1))
                dve.tensor_tensor(pm[:, :, :], pl[:, :, :], oh[:, :, :], ALU.mult).then_inc(v_pm, 1)
                wait(dve, v_pm, g.times(1, 1))
                wait(dve, d_tab, g.times(16 * GB))
                dve.tensor_copy(tid[:, :], tid_all[:, bass.ds(g.times(GB), GB)]).then_inc(v_tid, 1)
                with nc.allow_low_precision(reason="slot numbers are whole and far below 2**24"):
                    dve.tensor_reduce(pos[:, :], pm[:, :, :], AX_X, ALU.add).then_inc(v_pos, 1)

            steps(dve, step)


def expert_phase(nc, sb_in, sem, v):
    b2 = v["b2"]
    D, E, KC, F, FC, SL, NT, TS, NH, N = (v[n] for n in ("D", "E", "KC", "F", "FC", "SL", "NT", "TS", "NH", "N"))
    tab, rows, outf = v["tab"], v["rows"], v["outf"]
    bS, bC, bPV, bM0, bM1, bM2 = (v[n] for n in ("bS", "bC", "bPV", "bM0", "bM1", "bM2"))
    identf, b1t, halfneg, raw, d_raw, load_experts = (
        v[n] for n in ("identf", "b1t", "halfneg", "raw", "d_raw", "load_experts"))
    up_bank = [bS[0], bS[1], bC[0], bC[1]]
    down_bank = [bPV, bM2]
    turn_bank = [bM0, bM1]
    NU = 2 * FC
    TURNS = NT // 2
    PIECES = 8
    PC = 2 * KC * F // PIECES
    STATS_AT = 4
    assert KC * F == FC * D and TURNS % 2 == 1

    with ExitStack() as scope:
        sb = sb_in(scope)
        b2s = sb("b2s", [TS, E, D], F32)
        idx = sb("idx", [TS, E, NT], U32)
        idx_in = sb("idx_in", [TS, NT], U32)
        idx_out = sb("idx_out", [TS, NT], U32)
        xs = [sb(f"xs{q}", [TS, NT, ROW], F32) for q in range(2)]
        st = sb("st", [TS, NT, 6], F32)
        mv = sb("mv", [TS, NT, 2], F32)
        ve = sb("ve", [TS, NT], F32)
        rs = sb("rs", [TS, NT], F32)
        xn = sb("xne", [TS, NT, D], F32)
        xh = [sb(f"xh{q}", [P, KC, SL], F32R) for q in range(2)]
        xl = [sb(f"xl{q}", [P, KC, SL], F32R) for q in range(2)]
        wh = [sb(f"weh{q}", [P, 2 * KC * F], F32R) for q in range(2)]
        wl = [sb(f"wel{q}", [P, 2 * KC * F], F32R) for q in range(2)]
        gl = [sb(f"gl{i}", [P, NH], F32) for i in range(4)]
        hh = sb("hh", [P, FC, SL], F32R)
        hl = sb("hl", [P, FC, SL], F32R)
        yb = [sb(f"yb{j}", [TS, D], F32) for j in range(2)]
        ys = [sb(f"ys{j}", [TS, D], F32) for j in range(NT)]

        d_b2, d_idx, v_xs0 = sem("d_b2"), sem("d_idx"), sem("v_xs0")
        d_xs = [sem(f"d_xs{q}") for q in range(2)]
        d_out = [sem(f"d_out{j}") for j in range(NT)]
        e_turn, e_up, e_down = sem("e_turn"), sem("e_up"), sem("e_down")
        a_xh, a_weh, a_gelu, a_hh = sem("a_xh"), sem("a_weh"), sem("a_gelu"), sem("a_hh")
        v_est, v_emv, v_eve, v_exn, v_xl, v_wel, v_hl, v_yb, v_ys = (
            sem("v_" + n) for n in ("est", "emv", "eve", "exn", "xl", "wel", "hl", "yb", "ys"))
        p_ers, p_in, p_out = sem("p_ers"), sem("p_in"), sem("p_out")

        def expert(n, off):
            if isinstance(n, int) and not 0 <= off < E:
                return None
            return Turn(n, off, 2)

        def steps(eng, step):
            step(0, 0)
            step(0, 1)
            with eng.Fori(0, (E - 4) // 2) as n:
                for c in range(2):
                    step(n, 2 + c)
            step(0, E - 2)
            step(0, E - 1)

        block = scope.enter_context(nc.Block())

        @block.sync
        def _(sp):
            sp.dma_start(idx[:, :, :], tab[:, :].rearrange("(e p j) o -> p e (j o)", e=E, j=NT)).then_inc(d_idx, 16)
            sp.dma_start(b2s[:, :, :], b2.unsqueeze(0).to_broadcast([TS, E, D])).then_inc(d_b2, 16)

            def step(n, i):
                e = expert(n, i + 2)
                if e:
                    hold(sp, a_weh, e.back(1).times(PIECES))
                    hold(sp, v_wel, e.back(1).times(PIECES))
                    load_experts(sp, e.times(1), e.slot)

            steps(sp, step)
            for j in range(NT):
                sp.wait_ge(d_out[j], 16 * E)

        @block.gpsimd
        def _(pool):
            def tokens_in(e):
                if not (isinstance(e.n, int) and e.off == 0):
                    last = e.back(1)
                    hold(pool, d_xs[last.slot], last.round(16 * NT, 16 * NT))
                pool.tensor_copy(idx_in[:, :], idx[:, bass.ds(e.times(1), 1), :].rearrange("p a j -> p (a j)")
                                 ).then_inc(p_in, 1)
                hold(pool, p_in, e.times(1, 1))

            def tokens_out(e):
                for j in range(NT):
                    hold(pool, d_out[j], e.times(16))
                pool.tensor_copy(idx_out[:, :], idx[:, bass.ds(e.times(1), 1), :].rearrange("p a j -> p (a j)")
                                 ).then_inc(p_out, 1)
                hold(pool, p_out, e.times(1, 1))

            def fetch(e, j):
                pool.indirect_dma_start(out=xs[e.slot][:, j, :], out_offset=None, in_=rows[:, :],
                                        in_offset=bass.IndirectOffsetOnAxis(ap=idx_in[:, j:j + 1], axis=0),
                                        bounds_check=N - 1, oob_is_err=False).then_inc(d_xs[e.slot], 16)

            def scale_of(e):
                wait(pool, v_eve, e.times(1, 1))
                pool.tensor_tensor(rs[:, :], ve[:, :], halfneg[0:TS, 0:NT], ALU.pow).then_inc(p_ers, 1)

            pool.wait_ge(d_idx, 16)
            pool.wait_ge(v_xs0, 1)
            tokens_in(expert(0, 0))
            for j in range(NT):
                fetch(expert(0, 0), j)
            scale_of(expert(0, 0))
            pool.wait_ge(v_xs0, 2)
            tokens_in(expert(0, 1))
            for j in range(NT):
                fetch(expert(0, 1), j)

            def step(n, i):
                e, e1, e2 = expert(n, i), expert(n, i + 1), expert(n, i + 2)
                if e1:
                    scale_of(e1)
                tokens_out(e)
                if e2:
                    tokens_in(e2)
                for j in range(NT):
                    hold(pool, v_ys, e.times(NT, j + 1))
                    pool.indirect_dma_start(out=outf,
                                            out_offset=bass.IndirectOffsetOnAxis(ap=idx_out[:, j:j + 1], axis=0),
                                            in_=ys[j][:, :], in_offset=None,
                                            bounds_check=N - 1, oob_is_err=False).then_inc(d_out[j], 16)
                    if e2:
                        fetch(e2, j)

            steps(pool, step)

        @block.scalar
        def _(act):
            def split(e, c):
                q = e.slot
                wait(act, d_raw[q], e.round(32, 32))
                wait(act, e_down, e.back(1).times(NT))
                act.activation(wh[q][:, c * PC:(c + 1) * PC], raw[q][:, c * PC:(c + 1) * PC], ACT.Copy
                               ).then_inc(a_weh, 1)

            def turned(e, r):
                wait(act, e_turn, e.times(TURNS, r + 1))
                act.activation(xh[e.slot][:, :, 2 * r * TS:2 * (r + 1) * TS],
                               turn_bank[r % 2][:, 0:KC * 2 * TS].rearrange("p (k t) -> p k t", k=KC), ACT.Copy
                               ).then_inc(a_xh, 1)

            e0 = expert(0, 0)
            for c in range(PIECES):
                split(e0, c)
            for r in range(TURNS):
                turned(e0, r)

            def step(n, i):
                e, e1 = expert(n, i), expert(n, i + 1)

                def rounded(u):
                    half, f = divmod(u, FC)
                    cols = slice(half * NH, (half + 1) * NH)
                    wait(act, e_down, e.back(1).times(NT, (half + 1) * NT // 2))
                    wait(act, a_gelu, e.times(NU, u + 1))
                    act.activation(hh[:, f, cols], gl[u % 4][:, :], ACT.Copy).then_inc(a_hh, 1)

                for u in range(NU):
                    wait(act, e_up, e.times(NU, u + 1))
                    hold(act, v_hl, e.times(NU, u - 3))
                    act.activation(gl[u % 4][:, :], up_bank[u % 4][:, 0:NH], ACT.Gelu,
                                   bias=b1t[:, bass.ds(e.times(FC, u % FC), 1)]).then_inc(a_gelu, 1)
                    if u:
                        rounded(u - 1)
                rounded(NU - 1)
                if e1:
                    for r in range(TURNS):
                        split(e1, 2 * r)
                        split(e1, 2 * r + 1)
                        turned(e1, r)
                    for c in range(2 * TURNS, PIECES):
                        split(e1, c)

            steps(act, step)

        @block.tensor
        def _(pe):
            def turn(e, r):
                wait(pe, v_exn, e.times(NT, 2 * r + 2))
                wait(pe, v_xl, e.times(TURNS, r - 1 if r == 2 else r))
                for k in range(KC):
                    for j in range(2):
                        at = (k * 2 + j) * TS
                        last = pe.transpose(turn_bank[r % 2][:, at:at + TS], xn[:, 2 * r + j, k * P:(k + 1) * P],
                                            identf[0:TS, 0:TS])
                last.then_inc(e_turn, 1)

            for r in range(TURNS):
                turn(expert(0, 0), r)

            def step(n, i):
                e, e1 = expert(n, i), expert(n, i + 1)
                q = e.slot
                w1 = [w[q][:, 0:KC * F].rearrange("p (k f) -> p k f", k=KC) for w in (wh, wl)]
                w2 = [w[q][:, KC * F:].rearrange("p (c d) -> p c d", c=FC) for w in (wh, wl)]
                xt = [xh[q], xl[q]]
                ht = [hh, hl]
                three = ((0, 0), (0, 1), (1, 0))
                for u in range(NU):
                    half, f = divmod(u, FC)
                    wait(pe, v_xl, e.times(TURNS, TURNS))
                    wait(pe, v_wel, e.times(PIECES, PIECES // 2))
                    wait(pe, a_gelu, e.times(NU, u - 3))
                    terms = [(k, a, b) for k in range(KC) for a, b in three]
                    for m, (k, a, b) in enumerate(terms):
                        last = pe.matmul(up_bank[u % 4][:, 0:NH], w1[a][:, k, f * P:(f + 1) * P],
                                         xt[b][:, k, half * NH:(half + 1) * NH],
                                         start=(m == 0), stop=(m == len(terms) - 1))
                    last.then_inc(e_up, 1)
                for j in range(NT):
                    wait(pe, v_hl, e.times(NU, FC * (1 + j // (NT // 2))))
                    wait(pe, v_wel, e.times(PIECES, PIECES))
                    wait(pe, v_yb, e.times(NT, j - 1))
                    terms = [(c, a, b) for c in range(FC) for a, b in three]
                    for m, (c, a, b) in enumerate(terms):
                        last = pe.matmul(down_bank[j % 2][0:TS, 0:D], ht[a][:, c, j * TS:(j + 1) * TS],
                                         w2[b][:, c, :], start=(m == 0), stop=(m == len(terms) - 1))
                    last.then_inc(e_down, 1)
                    if e1 and j < TURNS:
                        turn(e1, j)

            steps(pe, step)

        @block.vector
        def _(dve):
            for q in range(2):
                dve.memset(xs[q][:, :, :], 0.0).then_inc(v_xs0, 1)

            def split(e, c):
                q = e.slot
                wait(dve, a_weh, e.times(PIECES, c + 1))
                dve.tensor_tensor(wl[q][:, c * PC:(c + 1) * PC], raw[q][:, c * PC:(c + 1) * PC],
                                  wh[q][:, c * PC:(c + 1) * PC].bitcast(F32), ALU.subtract).then_inc(v_wel, 1)

            def stats(e, j):
                if j == 0:
                    wait(dve, d_xs[e.slot], e.round(16 * NT, 16 * NT))
                    hold(dve, v_exn, e.times(NT))
                dve.bn_stats(st[:, j, :], xs[e.slot][:, j, 0:D]).then_inc(v_est, 1)

            def aggregate(e):
                hold(dve, v_est, e.times(NT, NT))
                for j in range(NT):
                    last = dve.bn_aggr(mv[:, j, :], st[:, j, :])
                last.then_inc(v_emv, 1)
                wait(dve, v_emv, e.times(1, 1))
                dve.tensor_scalar(ve[:, :], mv[:, :, 1], EPS, None, ALU.add).then_inc(v_eve, 1)

            def normalise(e, j):
                wait(dve, p_ers, e.times(1, 1))
                wait(dve, e_turn, e.times(TURNS))
                dve.tensor_scalar(xn[:, j, :], xs[e.slot][:, j, 0:D], mv[:, j, 0:1], rs[:, j:j + 1],
                                  ALU.subtract, ALU.mult).then_inc(v_exn, 1)

            def turned(e, r):
                wait(dve, a_xh, e.times(TURNS, r + 1))
                at = slice(2 * r * TS, 2 * (r + 1) * TS)
                dve.tensor_tensor(xl[e.slot][:, :, at],
                                  turn_bank[r % 2][:, 0:KC * 2 * TS].rearrange("p (k t) -> p k t", k=KC),
                                  xh[e.slot][:, :, at].bitcast(F32), ALU.subtract).then_inc(v_xl, 1)

            e0 = expert(0, 0)
            for c in range(PIECES):
                split(e0, c)
            for j in range(NT):
                stats(e0, j)
            aggregate(e0)
            for j in range(NT):
                normalise(e0, j)
            for r in range(TURNS):
                turned(e0, r)
            dve.wait_ge(d_b2, 16)

            def step(n, i):
                e, e1 = expert(n, i), expert(n, i + 1)
                for u in range(NU):
                    half, f = divmod(u, FC)
                    cols = slice(half * NH, (half + 1) * NH)
                    wait(dve, a_hh, e.times(NU, u + 1))
                    dve.tensor_tensor(hl[:, f, cols], gl[u % 4][:, :], hh[:, f, cols].bitcast(F32), ALU.subtract
                                      ).then_inc(v_hl, 1)
                    if e1 and STATS_AT <= u < STATS_AT + NT:
                        stats(e1, u - STATS_AT)
                    if e1 and u == STATS_AT + NT:
                        aggregate(e1)
                    if e1 and u >= NU - 3:
                        normalise(e1, 2 * (u - NU + 3))
                        normalise(e1, 2 * (u - NU + 3) + 1)
                if e1:
                    split(e1, 0)
                    split(e1, 1)
                for j in range(NT):
                    wait(dve, e_down, e.times(NT, j + 1))
                    wait(dve, v_ys, e.times(NT, j - 1))
                    dve.tensor_tensor(yb[j % 2][:, :], down_bank[j % 2][0:TS, 0:D],
                                      b2s[:, bass.ds(e.times(1), 1), :].rearrange("p a d -> p (a d)"), ALU.add
                                      ).then_inc(v_yb, 1)
                    wait(dve, v_yb, e.times(NT, j + 1))
                    wait(dve, d_out[j], e.times(16))
                    dve.scalar_tensor_tensor(out=ys[j][:, :], in0=yb[j % 2][:, :],
                                             scalar=xs[e.slot][:, j, D:D + 1], in1=xs[e.slot][:, j, 0:D],
                                             op0=ALU.mult, op1=ALU.add).then_inc(v_ys, 1)
                    if e1 and j < TURNS:
                        turned(e1, j)
                    if e1:
                        for c in ((2,), (3,), (4,), (5, 6), (7,), ())[j]:
                            split(e1, c)

            steps(dve, step)


_INS = ["x", "L0_tok_weight", "L0_attn_q_proj", "L0_attn_k_proj", "L0_attn_v_proj", "L0_attn_o_proj",
        "L0_ffn_wg", "L0_ffn_W1", "L0_ffn_b1", "L0_ffn_W2", "L0_ffn_b2"]


def kernel(**inputs):
    import numpy as _np
    import concourse.bacc as _bacc
    from concourse import mybir as _mybir
    from concourse.bass_utils import run_bass_kernel_spmd as _run

    nc = _bacc.Bacc("TRN2", target_bir_lowering=False, num_devices=1)
    arrays, args = {}, []
    for name in _INS:
        a = _np.ascontiguousarray(inputs[name])
        arrays[f"in_{name}_dram"] = a
        args.append(nc.dram_tensor(f"in_{name}_dram", a.shape, _mybir.dt.from_np(a.dtype), kind="ExternalInput").ap())
    nb, s = inputs["x"].shape
    d = inputs["L0_tok_weight"].shape[1]
    args.append(nc.dram_tensor("out_0_dram", (nb, s, d), _mybir.dt.float32, kind="ExternalOutput").ap())
    lm_block(nc, *args)
    r = _run(nc, [arrays], core_ids=[0])
    return r.results[0]["out_0_dram"]
```

```python
from contextlib import ExitStack

import concourse.bass as bass
from concourse import mybir

P = 128
F32 = mybir.dt.float32
F32R = mybir.dt.float32r
BF16 = mybir.dt.bfloat16
U32 = mybir.dt.uint32
I32 = mybir.dt.int32
ALU = mybir.AluOpType
ACT = mybir.ActivationFunctionType
AX_X = mybir.AxisListType.X

EPS = 1e-5
MASKED = -1e30
RING = 4
UNITS = 8
AHEAD = 6
ROW = 260


class Turn:

    def __init__(self, n, off, period):
        self.n, self.off, self.period = n, off, period
        self.slot = off % period

    def times(self, per, more=0):
        base = per * self.off + more
        return base if isinstance(self.n, int) else self.n * (per * self.period) + base

    def round(self, per, more=0):
        base = per * (self.off // self.period) + more
        return base if isinstance(self.n, int) else self.n * per + base

    def back(self, k):
        return Turn(self.n, self.off - k, self.period)


def wait(engine, semaphore, value):
    if isinstance(value, int) and value <= 0:
        return
    engine.wait_ge(semaphore, value)


def hold(engine, semaphore, value):
    wait(engine, semaphore, value)
    if not isinstance(value, int):
        engine.nop(nofuse=True)


def lm_block(nc, x, table, wq, wk, wv, wo, wg, W1, b1, W2, b2, out):
    NB, S = x.shape
    D = table.shape[1]
    E, _, F = W1.shape
    H, DK = 16, D // 16
    N = NB * S
    CAP = int(N / E * 1.25) + 1
    KC = D // P
    GB = 2
    NG = NB // GB
    GT = GB * S
    QUADS = H // 4
    PARTS = 3
    KS_ROWS = 6 * DK
    SCALE = float(DK) ** -0.5
    NT = 6
    TS = -(-CAP // NT)
    TS += TS % 2
    SL = NT * TS
    NH = SL // 2
    FC = F // P
    NOWHERE = 1 << 20
    assert S == P and TS <= P and NH <= 512

    tab = nc.dram_tensor("token_of_slot", [E * SL, 1], U32)
    rows = nc.dram_tensor("h_rows", [N, ROW], F32)
    qparts = [nc.dram_tensor(f"q_parts{i}", [PARTS, D, GT], BF16) for i in range(RING)]
    kparts = [nc.dram_tensor(f"k_parts{i}", [PARTS, D, GT], BF16) for i in range(RING)]
    outf = out.rearrange("b s d -> (b s) d")

    with ExitStack() as whole:
        def sb_in(scope):
            return lambda name, shape, dt: scope.enter_context(nc.sbuf_tensor(name, shape, dt))

        sb = sb_in(whole)

        def sem(name):
            return whole.enter_context(nc.semaphore(name))

        bank = {n: whole.enter_context(nc.psum_tensor(n, [P, 512], F32))
                for n in ("S0", "S1", "C0", "C1", "PV", "M0", "M1", "M2")}
        bS = [bank["S0"], bank["S1"]]
        bC = [bank["C0"], bank["C1"]]
        bPV, bM0, bM1, bM2 = bank["PV"], bank["M0"], bank["M1"], bank["M2"]

        identf = sb("identf", [P, P], F32)
        raw = [sb(f"w_raw{q}", [P, 2 * KC * F], F32) for q in range(2)]
        biases = sb("biases", [P, E * (FC + KC)], F32)
        halfneg = sb("halfneg", [P, 8], F32)
        idx = sb("idx", [TS, E, NT], U32)
        d_idx = sem("d_idx")
        d_raw = [sem(f"d_raw{q}") for q in range(2)]

        def load_experts(eng, e, q):
            eng.dma_start(raw[q][:, 0:KC * F].rearrange("p (k f) -> p k f", k=KC),
                          W1[bass.ds(e, 1)].rearrange("a (k p) f -> p (a k) f", p=P)).then_inc(d_raw[q], 16)
            eng.dma_start(raw[q][:, KC * F:].rearrange("p (c d) -> p c d", c=FC),
                          W2[bass.ds(e, 1)].rearrange("a (c p) d -> p (a c) d", p=P)).then_inc(d_raw[q], 16)

        attention_phase(nc, sb_in, sem, locals())
        expert_phase(nc, sb_in, sem, locals())


def attention_phase(nc, sb_in, sem, v):
    x, table, wq, wk, wv, wo, wg, b1, b2 = (v[n] for n in ("x", "table", "wq", "wk", "wv", "wo", "wg", "b1", "b2"))
    NB, S, D, E, H, DK, CAP, KC, GB, NG, GT, QUADS = (
        v[n] for n in ("NB", "S", "D", "E", "H", "DK", "CAP", "KC", "GB", "NG", "GT", "QUADS"))
    PARTS, KS_ROWS, SCALE, SL, FC, NOWHERE, N = (
        v[n] for n in ("PARTS", "KS_ROWS", "SCALE", "SL", "FC", "NOWHERE", "N"))
    tab, rows, qparts, kparts, outf, idx, d_idx, NT = (
        v[n] for n in ("tab", "rows", "qparts", "kparts", "outf", "idx", "d_idx", "NT"))
    bS, bC, bPV, bM0, bM1, bM2 = (v[n] for n in ("bS", "bC", "bPV", "bM0", "bM1", "bM2"))
    identf, biases, halfneg, raw, load_experts = (
        v[n] for n in ("identf", "biases", "halfneg", "raw", "load_experts"))
    BIG = float(NOWHERE)

    with ExitStack() as scope:
        sb = sb_in(scope)
        identb = sb("identb", [P, P], BF16)
        maskb = sb("maskb", [P, 4, S], BF16)
        trib = sb("trib", [P, P], BF16)
        onesb = sb("onesb", [P, P], BF16)
        eps_of = sb("eps_of", [P, GB * E], I32)
        iota8 = sb("iota8", [P, GB, E], F32)
        base = sb("base", [P, E], F32)
        limit = sb("limit", [P, E], F32)
        tid_all = sb("tid_all", [P, NB], U32)
        nowhere = sb("nowhere", [96, E * SL // 96], U32)
        wraw = raw[1][:, 0:4 * KC * D].rearrange("p (m c d) -> p m c d", m=4, c=KC)
        wh = [sb(f"wh{m}", [P, KC, D], F32R) for m in range(4)]
        wl = [sb(f"wl{m}", [P, KC, D], F32R) for m in range(4)]
        wgs = sb("wgs", [P, KC, E], F32)
        bias_raw = sb("bias_raw", [E * (FC + KC), P], F32)
        xi = sb("xi", [NB, S], I32)
        xf = sb("xf", [NB, S], F32)
        idt = sb("idt", [P, NB], U32)
        h = sb("h", [P, NB, ROW], F32)
        st1 = sb("st1", [P, GB, 6], F32)
        mv1 = sb("mv1", [P, GB, 2], F32)
        ve1 = sb("ve1", [P, GB], F32)
        rs1 = sb("rs1", [P, GB], F32)
        xn = sb("xn", [P, GB, D], F32)
        xth = sb("xth", [P, KC, GT], F32R)
        xtl = sb("xtl", [P, KC, GT], F32R)
        qp = sb("qp", [P, PARTS, KC, GT], BF16)
        kp = sb("kp", [P, PARTS, KC, GT], BF16)
        qr = sb("qr", [P, KC, GT], F32)
        kr = sb("kr", [P, KC, GT], F32)
        qs = [sb(f"qs{i}", [KS_ROWS + 1, H, GT], BF16) for i in range(RING)]
        ks = [sb(f"ks{i}", [KS_ROWS + 1, H, GT], BF16) for i in range(RING)]
        va = [sb(f"va{i}", [P, GB, H, 2 * DK], F32) for i in range(RING)]
        mx = [sb(f"mx{i}", [P, H, GB], F32) for i in range(RING)]
        nm = [sb(f"nm{i}", [GB * H, S], BF16) for i in range(RING)]
        pt = [sb(f"pt{i}", [P, 4, S], F32) for i in range(4)]
        osb = [sb(f"os{i}", [P, QUADS, S], F32) for i in range(GB)]
        rec = sb("rec", [P, GB, H], F32)
        on = sb("on", [P, GB, D], F32)
        oth = sb("oth", [P, KC, GT], F32R)
        otl = sb("otl", [P, KC, GT], F32R)
        st2 = sb("st2", [P, GB, 6], F32)
        mv2 = sb("mv2", [P, GB, 2], F32)
        ve2 = sb("ve2", [P, GB], F32)
        xn2 = sb("xn2", [P, GB, D], F32)
        x2t = sb("x2t", [P, KC, GT], F32)
        lmax = sb("lmax", [P, GB], F32)
        leq = sb("leq", [P, GB, E], F32)
        first = sb("first", [P, GB], F32)
        oh = sb("oh", [P, GB, E], BF16)
        dl = sb("dl", [P, GB, E], F32)
        ex = sb("ex", [P, GB, E], F32)
        se = sb("se", [P, GB], F32)
        cn = sb("cn", [P, GB, E], F32)
        over = sb("over", [P, GB, E], F32)
        pl = sb("pl", [P, GB, E], F32)
        pm = sb("pm", [P, GB, E], F32)
        pos = sb("pos", [P, GB], U32)
        tid = sb("tid", [P, GB], U32)

        d_x, d_w, d_c, d_init, d_ones, v_ones = (sem(n) for n in ("d_x", "d_w", "d_c", "d_init", "d_ones", "v_ones"))
        d_g = [sem(f"d_g{i}") for i in range(RING)]
        d_qw, d_kw = sem("d_qw"), sem("d_kw")
        d_q = [sem(f"d_q{i}") for i in range(RING)]
        d_k = [sem(f"d_k{i}") for i in range(RING)]
        d_sh = [sem(f"d_sh{i}") for i in range(RING)]
        d_rows, d_tab = sem("d_rows"), sem("d_tab")
        g_set, g_cst, v_cst = sem("g_set"), sem("g_cst"), sem("v_cst")
        v_xf, pe_id, v_idt, pe_w, a_wh, v_wl = (sem(n) for n in ("v_xf", "pe_id", "v_idt", "pe_w", "a_wh", "v_wl"))
        pe_bias, v_bias = sem("pe_bias"), sem("v_bias")
        pe_T, pe_Q, pe_K, pe_V, pe_S, pe_mT, pe_C, pe_PV, pe_OT, pe_oT, pe_O, pe_x2T, pe_lg, pe_rk = (
            sem("pe_" + n) for n in ("T", "Q", "K", "V", "S", "mT", "C", "PV", "OT", "oT", "O", "x2T", "lg", "rk"))
        a_xth, a_q1, a_q2, a_k1, a_k2, a_V, a_exp, a_nm, a_os, a_oth, a_x2t, a_ex = (
            sem("a_" + n) for n in ("xth", "q1", "q2", "k1", "k2", "V", "exp", "nm", "os", "oth", "x2t", "ex"))
        v_st1, v_mv1, v_ve1, v_xn, v_xtl, v_qr, v_kr, v_mx, v_rec, v_on, v_otl = (
            sem("v_" + n) for n in ("st1", "mv1", "ve1", "xn", "xtl", "qr", "kr", "mx", "rec", "on", "otl"))
        v_h1, v_st2, v_mv2, v_ve2, v_xn2, v_lmax, v_leq, v_first, v_dl, v_se, v_w = (
            sem("v_" + n) for n in ("h1", "st2", "mv2", "ve2", "xn2", "lmax", "leq", "first", "dl", "se", "w"))
        v_oh, v_cn, v_over, v_pl, v_pm, v_base, v_tid, v_pos = (
            sem("v_" + n) for n in ("oh", "cn", "over", "pl", "pm", "base", "tid", "pos"))
        p_q3, p_k3, p_sel, p_rs1, p_rs2 = (sem("p_" + n) for n in ("q3", "k3", "sel", "rs1", "rs2"))

        def group(n, off):
            if isinstance(n, int) and not 0 <= off < NG:
                return None
            return Turn(n, off, RING)

        FIRST = AHEAD + 1
        ROUNDS = (NG - 1 - FIRST) // RING
        AFTER = FIRST + RING * ROUNDS
        LAST = NG + AHEAD

        def steps(eng, step):
            for i in range(FIRST):
                step(0, i)
            with eng.Fori(0, ROUNDS) as n:
                for c in range(RING):
                    step(n, FIRST + c)
            for i in range(AFTER, LAST):
                step(0, i)

        def shift_unit(n, i, s, lag):
            d, u = divmod(s - lag, UNITS)
            return group(n, i + d), u

        S_LAG, C_LAG, PV_LAG = UNITS + 4, 2 * UNITS + 7, 3 * UNITS + 1

        def weight_columns(w, m):
            bank = (bM1, bM2, bS[0], bS[1])[m]
            if m > 1:
                return [(w[:, :, :], bank[:, :].rearrange("p (k d) -> p k d", k=KC))]
            return [(w[:, k, c * P:(c + 1) * P].rearrange("p (d j) -> p d j", d=DK),
                     bank[:, k * D:(k + 1) * D].rearrange("p (j c d) -> p c d j", c=KC, d=DK)[:, c])
                    for k in range(KC) for c in range(KC)]

        block = scope.enter_context(nc.Block())

        @block.sync
        def _(sp):
            sp.dma_start(xi[:, :], x).then_inc(d_x, 16)
            for m, w in enumerate((wq, wk, wv, wo)):
                sp.dma_start(wraw[:, m], w.rearrange("(c p) d -> p c d", p=P)).then_inc(d_w, 16)
            sp.dma_start(wgs[:, :, :], wg.rearrange("(k p) e -> p k e", p=P)).then_inc(d_c, 16)
            sp.dma_start(bias_raw[0:E * FC, :], b1.rearrange("e (c p) -> (e c) p", p=P)).then_inc(d_c, 16)
            sp.dma_start(bias_raw[E * FC:, :], b2.rearrange("e (c p) -> (e c) p", p=P)).then_inc(d_c, 16)
            sp.wait_ge(g_set, 1)
            sp.dma_start(tab[:, :].rearrange("(p n) o -> p (n o)", p=96), nowhere[:, :]).then_inc(d_init, 16)
            sp.wait_ge(v_ones, 1)
            for i in range(RING):
                sp.dma_start(ks[i][KS_ROWS:KS_ROWS + 1, :, :], onesb[0:H * GT // P, :]).then_inc(d_ones, 16)
            load_experts(sp, 0, 0)
            sp.wait_ge(pe_w, 4)
            load_experts(sp, 1, 1)

            def stacks_q(parts, stacked, done):
                at = 0
                for part, times in enumerate((3, 2, 1)):
                    sp.dma_start(stacked[at:at + times * DK, :, :],
                                 parts[part].rearrange("(d h) t -> d h t", d=DK).unsqueeze(0)
                                 .to_broadcast([times, DK, H, GT])).then_inc(done, 16)
                    at += times * DK

            def stacks_k(parts, stacked, done):
                at = 0
                for count in (3, 2, 1):
                    sp.dma_start(stacked[at:at + count * DK, :, :],
                                 parts[0:count].rearrange("a (d h) t -> (a d) h t", d=DK)).then_inc(done, 16)
                    at += count * DK

            def step(n, i):
                g = group(n, i)
                if g:
                    hold(sp, pe_C, g.back(RING - 1).times(UNITS))
                    hold(sp, p_q3, g.times(1, 1))
                    sp.dma_start(qparts[g.slot][:, :, :].rearrange("a (p k) t -> p a (k t)", p=P),
                                 qp[:, :, :, :].rearrange("p a k t -> p a (k t)")).then_inc(d_qw, 16)
                    hold(sp, p_k3, g.times(1, 1))
                    sp.dma_start(kparts[g.slot][:, :, :].rearrange("a (p k) t -> p a (k t)", p=P),
                                 kp[:, :, :, :].rearrange("p a k t -> p a (k t)")).then_inc(d_kw, 16)
                g2 = group(n, i - 2)
                if g2:
                    hold(sp, a_nm, g2.times(1, 1))
                    hold(sp, pe_C, g2.back(RING - 1).times(UNITS))
                    sp.dma_start(qs[g2.slot][KS_ROWS:KS_ROWS + 1, :, :].rearrange("p h (b t) -> p (h b) t", b=GB),
                                 nm[g2.slot][:, :]).then_inc(d_sh[g2.slot], 16)
                if g:
                    hold(sp, d_qw, g.times(16, 16))
                    stacks_q(qparts[g.slot], qs[g.slot], d_q[g.slot])
                    hold(sp, d_kw, g.times(16, 16))
                    stacks_k(kparts[g.slot], ks[g.slot], d_k[g.slot])
                g = group(n, i - 6)
                if g:
                    hold(sp, v_w, g.times(1, 1))
                    hg = h[:, bass.ds(g.times(GB), GB), :]
                    sp.dma_start(rows[bass.ds(g.times(GT), GT), :].rearrange("(b p) c -> p b c", p=P),
                                 hg).then_inc(d_rows, 16)
                    sp.dma_start(outf[bass.ds(g.times(GT), GT), :].rearrange("(b p) c -> p b c", p=P),
                                 hg[:, :, 0:D]).then_inc(d_rows, 16)

            steps(sp, step)
            sp.wait_ge(d_tab, 32 * NG)
            sp.dma_start(idx[:, :, :], tab[:, :].rearrange("(e p j) o -> p e (j o)", e=E, j=NT)).then_inc(d_idx, 16)
            sp.wait_ge(d_rows, 32 * NG)

        @block.gpsimd
        def _(pool):
            pool.memset(identf[:, :], 0.0).then_inc(g_cst, 1)
            pool.memset(nowhere[:, :], NOWHERE).then_inc(g_set, 1)
            pool.memset(maskb[:, :, :], 0.0).then_inc(g_cst, 1)
            pool.memset(trib[:, :], 1.0).then_inc(g_cst, 1)
            pool.wait_ge(g_cst, 3)
            pool.affine_select(out=identf[:, :], in_=identf[:, :], compare_op=ALU.not_equal, fill=1.0, base=0,
                               pattern=[[-1, P]], channel_multiplier=1).then_inc(g_set, 1)
            pool.affine_select(out=maskb[:, :, :], in_=maskb[:, :, :], compare_op=ALU.is_ge, fill=MASKED, base=0,
                               pattern=[[0, 4], [-1, S]], channel_multiplier=1).then_inc(g_set, 1)
            pool.affine_select(out=trib[:, :], in_=trib[:, :], compare_op=ALU.is_ge, fill=0.0, base=0,
                               pattern=[[1, P]], channel_multiplier=-1).then_inc(g_set, 1)
            pool.iota(eps_of[:, :], pattern=[[0, GB], [1, E]], base=0, channel_multiplier=0).then_inc(g_set, 1)
            pool.iota(tid_all[:, :], pattern=[[P, NB]], base=0, channel_multiplier=1).then_inc(g_set, 1)

            def store_slots(g, b):
                hold(pool, v_tid, g.times(1, 1))
                hold(pool, v_pos, g.times(1, 1))
                pool.indirect_dma_start(out=tab[:, :],
                                        out_offset=bass.IndirectOffsetOnAxis(ap=pos[:, b:b + 1], axis=0),
                                        in_=tid[:, b:b + 1], in_offset=None,
                                        bounds_check=E * SL - 1, oob_is_err=False).then_inc(d_tab, 16)

            def gather(g):
                wait(pool, d_g[g % RING], 16 * GB * (g // RING))
                for b in range(GB * g, GB * g + GB):
                    pool.indirect_dma_start(out=h[:, b, 0:D], out_offset=None, in_=table,
                                            in_offset=bass.IndirectOffsetOnAxis(ap=idt[:, b:b + 1], axis=0)
                                            ).then_inc(d_g[g % RING], 16)

            gathers = list(range(NG))
            pool.wait_ge(v_idt, 1)
            for g in gathers[:2]:
                gather(g)
            del gathers[:2]
            pool.wait_ge(v_cst, 3)
            pool.wait_ge(v_ve1, 1)
            pool.tensor_tensor(rs1[:, :], ve1[:, :], halfneg[:, 0:GB], ALU.pow).then_inc(p_rs1, 1)
            for g in gathers[:1]:
                gather(g)
            del gathers[:1]

            pool.wait_ge(d_init, 16)

            def step(n, i):
                for s in range(UNITS):
                    g, u = shift_unit(n, i, s, C_LAG)
                    if g:
                        buf = pt[u % 4]
                        hold(pool, a_exp, g.times(UNITS, u + 1))
                        pool.affine_select(out=buf[:, :, :], in_=buf[:, :, :], compare_op=ALU.is_ge, fill=0.0,
                                           base=0, pattern=[[0, 4], [1, S]], channel_multiplier=-1
                                           ).then_inc(p_sel, 1)
                    g = group(n, i)
                    if g and s == 2:
                        wait(pool, a_q2, g.times(1, 1))
                        pool.tensor_tensor(qp[:, 2], qr[:, :, :], qp[:, 1], ALU.subtract).then_inc(p_q3, 1)
                    if g and s == 3:
                        wait(pool, a_k2, g.times(1, 1))
                        pool.tensor_tensor(kp[:, 2], kr[:, :, :], kp[:, 1], ALU.subtract).then_inc(p_k3, 1)
                    g = group(n, i + 1)
                    if g and s == 5:
                        wait(pool, v_ve1, g.times(1, 1))
                        pool.tensor_tensor(rs1[:, :], ve1[:, :], halfneg[:, 0:GB], ALU.pow).then_inc(p_rs1, 1)
                    g = group(n, i - 4)
                    if g and s == 7:
                        wait(pool, v_ve2, g.times(1, 1))
                        pool.tensor_tensor(mv2[:, :, 1], ve2[:, :], halfneg[:, 0:GB], ALU.pow).then_inc(p_rs2, 1)
                    g = group(n, i - 6)
                    if g and s in (4, 6):
                        store_slots(g, s // 5)
                    if isinstance(n, int) and gathers and s in (6, 7):
                        gather(gathers.pop(0))
            steps(pool, step)

        @block.scalar
        def _(act):
            for m in range(4):
                act.wait_ge(pe_w, m + 1)
                for dst, src in weight_columns(wh[m], m):
                    last = act.activation(dst, src, ACT.Copy)
                last.then_inc(a_wh, 1)

            def step(n, i):
                def scores(s):
                    g, u = shift_unit(n, i, s, C_LAG)
                    if g:
                        wait(act, pe_C, g.times(UNITS, u + 1))
                        wait(act, pe_PV, g.times(UNITS, u - 3))
                        act.activation(pt[u % 4][:, :, :], bC[u % 2][:, :].rearrange("p (j t) -> p j t", j=4),
                                       ACT.Exp, scale=SCALE).then_inc(a_exp, 1)

                def values(g, b):
                    if g:
                        wait(act, pe_PV, g.times(UNITS, 4 * b + 4))
                        act.activation(osb[b][:, :, :], bPV[:, :].rearrange("p (a t) -> p a t", a=QUADS),
                                       ACT.Copy).then_inc(a_os, 1)

                def first_part(g, done, src, parts, w_done, first_done):
                    wait(act, done, g.times(1, 1))
                    wait(act, w_done, g.times(16))
                    act.activation(parts[:, 0], src[:, :].rearrange("p (k t) -> p k t", k=KC), ACT.Copy
                                   ).then_inc(first_done, 1)

                def second_part(g, rest_done, parts, rest, second_done):
                    wait(act, rest_done, g.times(1, 1))
                    act.activation(parts[:, 1], rest[:, :, :], ACT.Copy).then_inc(second_done, 1)

                def from_bank(dst, src, done, g, signal):
                    wait(act, done, g.times(1, 1))
                    act.activation(dst[:, :, :], src[:, :].rearrange("p (k t) -> p k t", k=KC), ACT.Copy
                                   ).then_inc(signal, 1)

                g0, g2, g3, g4, g5, g6 = (group(n, i - k) for k in (0, 2, 3, 4, 5, 6))
                if g0:
                    from_bank(xth, bM0, pe_T, g0, a_xth)
                scores(0)
                if g6:
                    wait(act, v_dl, g6.times(1, 1))
                    act.activation(ex[:, :, :], dl[:, :, :], ACT.Exp).then_inc(a_ex, 1)
                values(g4, 1)
                scores(1)
                if g0:
                    first_part(g0, pe_Q, bM0, qp, d_qw, a_q1)
                scores(2)
                if g0:
                    second_part(g0, v_qr, qp, qr, a_q2)
                if g0:
                    first_part(g0, pe_K, bM2, kp, d_kw, a_k1)
                scores(3)
                if g4:
                    from_bank(oth, bM1, pe_oT, g4, a_oth)
                if g0:
                    second_part(g0, v_kr, kp, kr, a_k2)
                scores(4)
                if g2:
                    wait(act, pe_mT, g2.times(1, 1))
                    act.activation(nm[g2.slot][:, :], bM2[0:GB * H, 0:S], ACT.Copy, scale=-1.0).then_inc(a_nm, 1)
                values(g3, 0)
                scores(5)
                if g5:
                    from_bank(x2t, bM2, pe_x2T, g5, a_x2t)
                scores(6)
                scores(7)
                if g0:
                    wait(act, pe_V, g0.times(1, 1))
                    wait(act, pe_PV, g0.back(RING - 1).times(UNITS))
                    act.activation(va[g0.slot][:, :, :, 0:DK].rearrange("p b h d -> p (b h) d"),
                                   bM1[:, :].rearrange("p (c d) -> p c d", d=DK), ACT.Copy).then_inc(a_V, 1)

            steps(act, step)

        @block.tensor
        def _(pe):
            def turn4(dst, src):
                for k in range(KC):
                    for b in range(GB):
                        at = (k * GB + b) * P
                        last = pe.transpose(dst[:, at:at + P], src[:, b, k * P:(k + 1) * P], identf[:, :])
                return last

            pe.wait_ge(g_set, 2)
            pe.wait_ge(v_xf, 1)
            pe.transpose(bM0[:, 0:NB], xf[:, :], identf[0:NB, 0:NB]).then_inc(pe_id, 1)
            pe.wait_ge(d_w, 64)
            for m in range(4):
                dst = [bM1, bM2, bS[0], bS[1]][m]
                for k in range(KC):
                    for c in range(KC):
                        last = pe.transpose(dst[:, k * D + c * P:k * D + (c + 1) * P],
                                            wraw[:, m, c, k * P:(k + 1) * P], identf[:, :])
                last.then_inc(pe_w, 1)
            pe.wait_ge(d_c, 48)
            pe.transpose(bC[0][:, 0:E * (FC + KC)], bias_raw[:, :], identf[0:E * (FC + KC), 0:E * (FC + KC)]
                         ).then_inc(pe_bias, 1)
            pe.wait_ge(v_idt, 1)
            pe.wait_ge(v_xn, 1)
            turn4(bM0, xn).then_inc(pe_T, 1)
            pe.wait_ge(a_wh, 4)
            pe.wait_ge(v_wl, 4)
            pe.wait_ge(v_idt, 1)
            pe.wait_ge(v_bias, 1)
            pe.wait_ge(v_cst, 6)
            pe.wait_ge(v_ones, 1)
            pe.wait_ge(d_ones, 16 * RING)
            pe.wait_ge(g_set, 6)

            def passes(dst, lhs, rhs):
                pairs = [(a, b) for k in range(KC) for a, b in ((0, 0), (0, 1), (1, 0))]
                for m, (a, b) in enumerate(pairs):
                    k = m // 3
                    last = pe.matmul(dst, lhs[a](k), rhs[b](k), start=(m == 0), stop=(m == len(pairs) - 1))
                return last

            def project(dst, m):
                for c in range(KC):
                    last = passes(dst[:, c * GT:(c + 1) * GT],
                                  [lambda k, w=w, c=c: w[m][:, k, c * P:(c + 1) * P] for w in (wh, wl)],
                                  [lambda k, t=t: t[:, k, :] for t in (xth, xtl)])
                return last

            def turn_values(dst, g, b):
                wait(pe, a_os, g.times(GB, b + 1))
                for a in range(QUADS):
                    last = pe.transpose(dst[:, a * P:(a + 1) * P], osb[b][:, a, :], identf[:, :])
                last.then_inc(pe_OT, 1)

            def step(n, i):
                for s in range(UNITS):
                    g, u = shift_unit(n, i, s, S_LAG)
                    if g:
                        if u == 0:
                            wait(pe, d_q[g.slot], g.round(48, 48))
                            wait(pe, d_k[g.slot], g.round(48, 48))
                        dst, b = bS[u % 2], u // QUADS
                        wait(pe, v_mx, g.times(UNITS, u - 1))
                        pe.matmul(dst[:, :], identb[:, :], maskb[:, :, :], start=True, stop=False)
                        for j in range(4):
                            hh = (u % QUADS) * 4 + j
                            last = pe.matmul(dst[:, j * S:(j + 1) * S],
                                             qs[g.slot][0:KS_ROWS, hh, b * S:(b + 1) * S],
                                             ks[g.slot][0:KS_ROWS, hh, b * S:(b + 1) * S],
                                             start=False, stop=(j == 3))
                        last.then_inc(pe_S, 1)
                    g, u = shift_unit(n, i, s, C_LAG)
                    if g:
                        if u == 0:
                            wait(pe, d_sh[g.slot], g.round(16, 16))
                        b = u // QUADS
                        wait(pe, a_exp, g.times(UNITS, u - 1))
                        for j in range(4):
                            hh = (u % QUADS) * 4 + j
                            last = pe.matmul(bC[u % 2][:, j * S:(j + 1) * S],
                                             ks[g.slot][:, hh, b * S:(b + 1) * S],
                                             qs[g.slot][:, hh, b * S:(b + 1) * S], start=True, stop=True)
                        last.then_inc(pe_C, 1)
                    g = group(n, i - 4)
                    if g and s == 2:
                        wait(pe, v_h1, g.times(1))
                        wait(pe, a_V, g.times(1, 4) if group(n, i - 1) else NG)
                        turn_values(bM1, g, 1)
                    if g and s == 3:
                        wait(pe, v_on, g.times(GB, GB))
                        turn4(bM1, on).then_inc(pe_oT, 1)
                    g = group(n, i)
                    if g and s == 2:
                        wait(pe, a_nm, g.back(3).times(1, 1))
                        wait(pe, v_base, g.back(6).times(1, 2))
                        project(bM2, 1).then_inc(pe_K, 1)
                    if g and s == 7:
                        wait(pe, v_h1, g.back(4).times(1, 1))
                        wait(pe, a_V, g.times(1))
                        for b in range(GB):
                            last = passes(bM1[:, b * D:(b + 1) * D],
                                          [lambda k, t=t, b=b: t[:, k, b * S:(b + 1) * S] for t in (xth, xtl)],
                                          [lambda k, w=w: w[2][:, k, :] for w in (wh, wl)])
                        last.then_inc(pe_V, 1)
                    g = group(n, i + 1)
                    if g and s == 7:
                        wait(pe, v_xn, g.times(1, 1))
                        wait(pe, v_qr, g.times(1))
                        wait(pe, v_on, g.back(4).times(GB, 1))
                        turn4(bM0, xn).then_inc(pe_T, 1)
                    g = group(n, i - 2)
                    if g and s == 4:
                        wait(pe, v_mx, g.times(UNITS, UNITS))
                        wait(pe, a_k1, g.times(1, 3) if group(n, i) else NG)
                        wait(pe, v_kr, g.times(1, 3) if group(n, i) else NG)
                        wait(pe, v_base, g.back(4).times(1, 2))
                        pe.transpose(bM2[0:GB * H, 0:S], mx[g.slot][:, :, :].rearrange("p h b -> p (h b)"), identf[:, :]).then_inc(pe_mT, 1)
                    g = group(n, i - 4)
                    if g and s == 5:
                        wait(pe, a_oth, g.times(1, 1))
                        wait(pe, v_otl, g.times(1, 1))
                        for b in range(GB):
                            last = passes(bM1[:, b * D:(b + 1) * D],
                                          [lambda k, t=t, b=b: t[:, k, b * S:(b + 1) * S] for t in (oth, otl)],
                                          [lambda k, w=w: w[3][:, k, :] for w in (wh, wl)])
                        last.then_inc(pe_O, 1)
                    g = group(n, i - 5)
                    if g and s == 5:
                        wait(pe, v_xn2, g.times(1, 1))
                        wait(pe, v_base, g.times(1, 1))
                        wait(pe, a_nm, g.times(1, 4) if group(n, i - 2) else NG)
                        turn4(bM2, xn2).then_inc(pe_x2T, 1)
                    if g and s == 6:
                        wait(pe, a_x2t, g.times(1, 1))
                        for b in range(GB):
                            for k in range(KC):
                                last = pe.matmul(bM2[:, b * E:(b + 1) * E], x2t[:, k, b * S:(b + 1) * S],
                                                 wgs[:, k, :], start=(k == 0), stop=(k == KC - 1))
                        last.then_inc(pe_lg, 1)
                    g = group(n, i - 6)
                    if g and s == 1:
                        wait(pe, v_oh, g.times(1, 1))
                        wait(pe, v_dl, g.times(1, 1))
                        pe.matmul(bM2[:, 0:E], trib[:, :], oh[:, 0, :], start=True, stop=True)
                        pe.matmul(bM2[:, E:2 * E], trib[:, :], oh[:, 1, :], start=True, stop=False)
                        pe.matmul(bM2[:, E:2 * E], onesb[:, :], oh[:, 0, :], start=False, stop=True)
                        pe.matmul(bM2[:, 2 * E:3 * E], onesb[:, :], oh[:, 0, :], start=True, stop=False)
                        pe.matmul(bM2[:, 2 * E:3 * E], onesb[:, :], oh[:, 1, :], start=False, stop=True
                                  ).then_inc(pe_rk, 1)
                    g = group(n, i)
                    if g and s == 1:
                        wait(pe, a_xth, g.times(1, 1))
                        wait(pe, v_xtl, g.times(1, 1))
                        project(bM0, 0).then_inc(pe_Q, 1)
                    g = group(n, i - 3)
                    if g and s == 6:
                        wait(pe, a_q1, g.times(1, 4) if group(n, i) else NG)
                        wait(pe, v_qr, g.times(1, 4) if group(n, i) else NG)
                        wait(pe, v_on, g.times(GB, -1))
                        turn_values(bM0, g, 0)
                    g, u = shift_unit(n, i, s, PV_LAG)
                    if g:
                        b = u // QUADS
                        if u == 0:
                            wait(pe, a_V, g.times(1, 1))
                        if u % QUADS == 0:
                            wait(pe, a_os, g.times(GB, b))
                        wait(pe, p_sel, g.times(UNITS, u + 1))
                        for j in range(4):
                            hh = (u % QUADS) * 4 + j
                            last = pe.matmul(bPV[32 * j:32 * j + 32, (u % QUADS) * S:(u % QUADS + 1) * S],
                                             va[g.slot][:, b, hh, :], pt[u % 4][:, j, :], start=True, stop=True)
                        last.then_inc(pe_PV, 1)

            steps(pe, step)

        @block.vector
        def _(dve):
            dve.wait_ge(d_x, 16)
            dve.tensor_copy(xf[:, :], xi[:, :]).then_inc(v_xf, 1)
            dve.memset(halfneg[:, :], -0.5).then_inc(v_cst, 1)
            dve.memset(onesb[:, :], 1.0).then_inc(v_ones, 1)
            dve.memset(h[:, :, D:ROW], 0.0).then_inc(v_cst, 1)
            dve.wait_ge(g_set, 2)
            dve.tensor_copy(identb[:, :], identf[:, :]).then_inc(v_cst, 1)
            dve.wait_ge(pe_id, 1)
            dve.tensor_copy(idt[:, :], bM0[:, 0:NB]).then_inc(v_idt, 1)
            for i in range(RING):
                last = dve.memset(va[i][:, :, :, DK:2 * DK], 1.0)
            last.then_inc(v_cst, 1)
            dve.wait_ge(g_set, 6)
            dve.tensor_scalar(iota8[:, :, :], eps_of[:, :].rearrange("p (b e) -> p b e", b=GB), -float(E), None,
                              ALU.add).then_inc(v_cst, 1)
            dve.tensor_scalar(base[:, :], eps_of[:, 0:E], float(SL), -1.0, ALU.mult, ALU.add).then_inc(v_base, 1)
            dve.tensor_scalar(limit[:, :], eps_of[:, 0:E], float(SL), float(CAP - 1), ALU.mult, ALU.add
                              ).then_inc(v_cst, 1)
            def low_weights(m):
                dve.wait_ge(a_wh, m + 1)
                for (dst, src), (high, _) in zip(weight_columns(wl[m], m), weight_columns(wh[m], m)):
                    last = dve.tensor_tensor(dst, src, high.bitcast(F32), ALU.subtract)
                last.then_inc(v_wl, 1)

            def stats(g, st, mv, ve, s_st, s_mv, s_ve):
                for b in range(GB):
                    last = dve.bn_stats(st[:, b, :], h[:, bass.ds(g.times(GB, b), 1), 0:D].rearrange("p a d -> p (a d)"))
                last.then_inc(s_st, 1)
                hold(dve, s_st, g.times(1, 1))
                for b in range(GB):
                    last = dve.bn_aggr(mv[:, b, :], st[:, b, :])
                last.then_inc(s_mv, 1)
                wait(dve, s_mv, g.times(1, 1))
                dve.tensor_scalar(ve[:, :], mv[:, :, 1], EPS, None, ALU.add).then_inc(s_ve, 1)

            def normalise(g, dst, mv, rs, done):
                for b in range(GB):
                    last = dve.tensor_scalar(dst[:, b, :],
                                             h[:, bass.ds(g.times(GB, b), 1), 0:D].rearrange("p a d -> p (a d)"),
                                             mv[:, b, 0:1], rs(b), ALU.subtract, ALU.mult)
                last.then_inc(done, 1)

            def stats1(g):
                wait(dve, d_g[g.slot], g.round(16 * GB, 16 * GB))
                hold(dve, v_xn, g.times(1))
                stats(g, st1, mv1, ve1, v_st1, v_mv1, v_ve1)

            def norm1(g):
                wait(dve, p_rs1, g.times(1, 1))
                normalise(g, xn, mv1, lambda b: rs1[:, b:b + 1], v_xn)

            g0 = group(0, 0)
            stats1(g0)
            low_weights(0)
            norm1(g0)
            for m in (1, 2, 3):
                low_weights(m)
            dve.wait_ge(pe_bias, 1)
            dve.tensor_copy(biases[:, :], bC[0][:, 0:E * (FC + KC)]).then_inc(v_bias, 1)
            dve.wait_ge(v_cst, 6)

            def step(n, i):
                def maxima(s):
                    g, u = shift_unit(n, i, s, S_LAG)
                    if g:
                        wait(dve, pe_S, g.times(UNITS, u + 1))
                        dve.tensor_reduce(mx[g.slot][:, 4 * (u % QUADS):4 * (u % QUADS) + 4, u // QUADS],
                                          bS[u % 2][:, :].rearrange("p (j t) -> p j t", j=4), AX_X, ALU.max
                                          ).then_inc(v_mx, 1)

                def low_part(g, dst, src, high, high_done, signal):
                    wait(dve, high_done, g.times(1, 1))
                    dve.tensor_tensor(dst[:, :, :], src[:, :].rearrange("p (k t) -> p k t", k=KC),
                                      high[:, :, :].bitcast(F32), ALU.subtract).then_inc(signal, 1)

                def rest_of(g, src, parts, rest, first_done, third_done, rest_done):
                    wait(dve, first_done, g.times(1, 1))
                    wait(dve, third_done, g.times(1))
                    dve.tensor_tensor(rest[:, :, :], src[:, :].rearrange("p (k t) -> p k t", k=KC), parts[:, 0],
                                      ALU.subtract).then_inc(rest_done, 1)

                def divide(g, b, bank):
                    src = bank[:, :].rearrange("p (h c) -> p h c", h=H)
                    wait(dve, pe_OT, g.times(GB, b + 1))
                    dve.reciprocal(rec[:, b, :], src[:, :, DK]).then_inc(v_rec, 1)
                    wait(dve, v_rec, g.times(GB, b + 1))
                    dve.tensor_tensor(on[:, b, :].rearrange("p (h d) -> p h d", h=H), src[:, :, 0:DK],
                                      rec[:, b, :].unsqueeze(2).to_broadcast([P, H, DK]), ALU.mult
                                      ).then_inc(v_on, 1)

                def second_norm(g):
                    if g:
                        wait(dve, p_rs2, g.times(1, 1))
                        dve.tensor_copy(h[:, bass.ds(g.times(GB), GB), D + 1:D + 3], mv2[:, :, :])
                        normalise(g, xn2, mv2, lambda b: mv2[:, b, 1:2], v_xn2)

                g0, g3, g4, g5, g6, nxt = (group(n, i - k) for k in (0, 3, 4, 5, 6, -1))
                if g0:
                    low_part(g0, xtl, bM0, xth, a_xth, v_xtl)
                maxima(0)
                if g6:
                    weigh(g6)
                if not g4:
                    second_norm(g5)
                maxima(1)
                if g6:
                    place(g6)
                if g0:
                    rest_of(g0, bM0, qp, qr, a_q1, p_q3, v_qr)
                maxima(2)
                if g4:
                    divide(g4, 1, bM1)
                if g0:
                    rest_of(g0, bM2, kp, kr, a_k1, p_k3, v_kr)
                maxima(3)
                if g4:
                    low_part(g4, otl, bM1, oth, a_oth, v_otl)
                if g4:
                    second_norm(g5)
                maxima(4)
                if nxt:
                    stats1(nxt)
                maxima(5)
                if g4:
                    wait(dve, pe_O, g4.times(1, 1))
                    hg = h[:, bass.ds(g4.times(GB), GB), 0:D]
                    dve.tensor_tensor(hg, bM1[:, :].rearrange("p (b d) -> p b d", b=GB), hg, ALU.add
                                      ).then_inc(v_h1, 1)
                if nxt:
                    norm1(nxt)
                maxima(6)
                if g3:
                    divide(g3, 0, bM0)
                if g4:
                    wait(dve, v_h1, g4.times(1, 1))
                    hold(dve, v_xn2, g4.times(1))
                    stats(g4, st2, mv2, ve2, v_st2, v_mv2, v_ve2)
                maxima(7)
                if g5:
                    route(g5)

            def spread(t):
                return t[:, :].unsqueeze(2).to_broadcast([P, GB, E])

            def route(g):
                lg = bM2[:, 0:GB * E].rearrange("p (b e) -> p b e", b=GB)
                wait(dve, pe_lg, g.times(1, 1))
                dve.tensor_reduce(lmax[:, :], lg, AX_X, ALU.max).then_inc(v_lmax, 1)
                wait(dve, v_lmax, g.times(1, 1))
                dve.tensor_tensor(leq[:, :, :], lg, spread(lmax), ALU.is_equal).then_inc(v_leq, 1)
                dve.tensor_tensor(dl[:, :, :], lg, spread(lmax), ALU.subtract).then_inc(v_dl, 1)
                wait(dve, v_leq, g.times(2, 1))
                dve.tensor_tensor(leq[:, :, :], leq[:, :, :], iota8[:, :, :], ALU.mult).then_inc(v_leq, 1)
                wait(dve, v_leq, g.times(2, 2))
                dve.tensor_reduce(first[:, :], leq[:, :, :], AX_X, ALU.min).then_inc(v_first, 1)
                wait(dve, v_first, g.times(1, 1))
                dve.tensor_tensor(oh[:, :, :], iota8[:, :, :], spread(first), ALU.is_equal).then_inc(v_oh, 1)

            def weigh(g):
                wait(dve, a_ex, g.times(1, 1))
                dve.tensor_reduce(se[:, :], ex[:, :, :], AX_X, ALU.add).then_inc(v_se, 1)
                wait(dve, v_se, g.times(1, 1))
                dve.reciprocal(h[:, bass.ds(g.times(GB), GB), D], se[:, :]).then_inc(v_w, 1)

            def place(g):
                wait(dve, pe_rk, g.times(1, 1))
                wait(dve, v_base, g.times(1, 1))
                rk = bM2[:, 0:GB * E].rearrange("p (b e) -> p b e", b=GB)
                dve.tensor_tensor(cn[:, :, :], rk, base[:, :].unsqueeze(1).to_broadcast([P, GB, E]), ALU.add
                                  ).then_inc(v_cn, 1)
                wait(dve, v_cn, g.times(1, 1))
                dve.tensor_tensor(base[:, :], bM2[:, GB * E:(GB + 1) * E], base[:, :], ALU.add).then_inc(v_base, 1)
                dve.tensor_tensor(over[:, :, :], cn[:, :, :], limit[:, :].unsqueeze(1).to_broadcast([P, GB, E]),
                                  ALU.is_gt).then_inc(v_over, 1)
                wait(dve, v_over, g.times(1, 1))
                dve.scalar_tensor_tensor(out=pl[:, :, :], in0=over[:, :, :], scalar=BIG, in1=cn[:, :, :],
                                         op0=ALU.mult, op1=ALU.add).then_inc(v_pl, 1)
                wait(dve, v_pl, g.times(1, 1))
                dve.tensor_tensor(pm[:, :, :], pl[:, :, :], oh[:, :, :], ALU.mult).then_inc(v_pm, 1)
                wait(dve, v_pm, g.times(1, 1))
                wait(dve, d_tab, g.times(16 * GB))
                dve.tensor_copy(tid[:, :], tid_all[:, bass.ds(g.times(GB), GB)]).then_inc(v_tid, 1)
                with nc.allow_low_precision(reason="slot numbers are whole and far below 2**24"):
                    dve.tensor_reduce(pos[:, :], pm[:, :, :], AX_X, ALU.add).then_inc(v_pos, 1)

            steps(dve, step)


def expert_phase(nc, sb_in, sem, v):
    D, E, KC, F, FC, SL, NT, TS, NH, N = (v[n] for n in ("D", "E", "KC", "F", "FC", "SL", "NT", "TS", "NH", "N"))
    rows, outf, idx, d_idx = v["rows"], v["outf"], v["idx"], v["d_idx"]
    bS, bC, bPV, bM0, bM1, bM2 = (v[n] for n in ("bS", "bC", "bPV", "bM0", "bM1", "bM2"))
    identf, biases, raw, d_raw, load_experts = (v[n] for n in ("identf", "biases", "raw", "d_raw", "load_experts"))
    up_bank = [bS[0], bS[1], bC[0], bC[1]]
    down_bank = [bPV, bM2]
    turn_bank = [bM0, bM1]
    back_bank = [bC[0], bC[1]]
    NU = 2 * FC
    DOWN = 2 * KC
    TURNS = NT // 2
    PIECES = 8
    PC = 2 * KC * F // PIECES
    assert KC * F == FC * D and TURNS % 2 == 1

    with ExitStack() as scope:
        sb = sb_in(scope)
        idx_in = sb("idx_in", [TS, NT], U32)
        idx_out = sb("idx_out", [TS, NT], U32)
        xs = [sb(f"xs{q}", [TS, NT, ROW], F32) for q in range(2)]
        xn = sb("xne", [TS, NT, D], F32)
        xh = [sb(f"xh{q}", [P, KC, SL], F32R) for q in range(2)]
        xl = [sb(f"xl{q}", [P, KC, SL], F32R) for q in range(2)]
        wh = [sb(f"weh{q}", [P, 2 * KC * F], F32R) for q in range(2)]
        wl = [sb(f"wel{q}", [P, 2 * KC * F], F32R) for q in range(2)]
        gl = [sb(f"gl{i}", [P, NH], F32) for i in range(4)]
        hh = sb("hh", [P, FC, SL], F32R)
        hl = sb("hl", [P, FC, SL], F32R)
        yt = sb("yt", [P, KC, SL], F32)
        ys = [sb(f"ys{j}", [TS, D], F32) for j in range(NT)]

        v_xs0 = sem("v_xs0")
        d_xs = [[sem(f"d_xs{q}_{j}") for j in range(NT)] for q in range(2)]
        d_out = [sem(f"d_out{j}") for j in range(NT)]
        e_turn, e_up, e_down, e_back = sem("e_turn"), sem("e_up"), sem("e_down"), sem("e_back")
        a_xh, a_weh, a_gelu, a_hh, a_yt = (sem("a_" + n) for n in ("xh", "weh", "gelu", "hh", "yt"))
        v_exn, v_xl, v_wel, v_hl, v_ys = (sem("v_" + n) for n in ("exn", "xl", "wel", "hl", "ys"))
        p_in, p_out = sem("p_in"), sem("p_out")

        def expert(n, off):
            if isinstance(n, int) and not 0 <= off < E:
                return None
            return Turn(n, off, 2)

        def steps(eng, step):
            step(0, 0)
            step(0, 1)
            with eng.Fori(0, (E - 4) // 2) as n:
                for c in range(2):
                    step(n, 2 + c)
            step(0, E - 2)
            step(0, E - 1)

        block = scope.enter_context(nc.Block())

        @block.sync
        def _(sp):
            for j in range(NT):
                sp.wait_ge(d_xs[0][j], 16)

            def step(n, i):
                e = expert(n, i + 2)
                if e:
                    hold(sp, a_weh, e.back(1).times(PIECES))
                    hold(sp, v_wel, e.back(1).times(PIECES))
                    load_experts(sp, e.times(1), e.slot)

            steps(sp, step)
            for j in range(NT):
                sp.wait_ge(d_out[j], 16 * E)

        @block.gpsimd
        def _(pool):
            def tokens_in(e):
                if not (isinstance(e.n, int) and e.off == 0):
                    last = e.back(1)
                    for j in range(NT):
                        hold(pool, d_xs[last.slot][j], last.round(16, 16))
                pool.tensor_copy(idx_in[:, :], idx[:, bass.ds(e.times(1), 1), :].rearrange("p a j -> p (a j)")
                                 ).then_inc(p_in, 1)
                hold(pool, p_in, e.times(1, 1))

            def tokens_out(e):
                for j in range(NT):
                    hold(pool, d_out[j], e.times(16))
                pool.tensor_copy(idx_out[:, :], idx[:, bass.ds(e.times(1), 1), :].rearrange("p a j -> p (a j)")
                                 ).then_inc(p_out, 1)
                hold(pool, p_out, e.times(1, 1))

            def fetch(e, j):
                pool.indirect_dma_start(out=xs[e.slot][:, j, :], out_offset=None, in_=rows[:, :],
                                        in_offset=bass.IndirectOffsetOnAxis(ap=idx_in[:, j:j + 1], axis=0),
                                        bounds_check=N - 1, oob_is_err=False).then_inc(d_xs[e.slot][j], 16)

            pool.wait_ge(d_idx, 16)
            pool.wait_ge(v_xs0, 1)
            tokens_in(expert(0, 0))
            for j in range(NT):
                fetch(expert(0, 0), j)
            pool.wait_ge(v_xs0, 2)
            tokens_in(expert(0, 1))
            for j in range(NT):
                fetch(expert(0, 1), j)

            def step(n, i):
                e, e2 = expert(n, i), expert(n, i + 2)
                tokens_out(e)
                if e2:
                    tokens_in(e2)
                for j in range(NT):
                    hold(pool, v_ys, e.times(NT, j + 1))
                    pool.indirect_dma_start(out=outf,
                                            out_offset=bass.IndirectOffsetOnAxis(ap=idx_out[:, j:j + 1], axis=0),
                                            in_=ys[j][:, :], in_offset=None,
                                            bounds_check=N - 1, oob_is_err=False).then_inc(d_out[j], 16)
                    if e2:
                        fetch(e2, j)

            steps(pool, step)

        @block.scalar
        def _(act):
            def split(e, c):
                q = e.slot
                wait(act, d_raw[q], e.round(32, 32))
                wait(act, e_down, e.back(1).times(DOWN))
                act.activation(wh[q][:, c * PC:(c + 1) * PC], raw[q][:, c * PC:(c + 1) * PC], ACT.Copy
                               ).then_inc(a_weh, 1)

            def turned(e, r):
                wait(act, e_turn, e.times(TURNS, r + 1))
                act.activation(xh[e.slot][:, :, 2 * r * TS:2 * (r + 1) * TS],
                               turn_bank[r % 2][:, 0:KC * 2 * TS].rearrange("p (k t) -> p k t", k=KC), ACT.Copy
                               ).then_inc(a_xh, 1)

            e0 = expert(0, 0)
            for c in range(PIECES):
                split(e0, c)
            for r in range(TURNS):
                turned(e0, r)

            def step(n, i):
                e, e1 = expert(n, i), expert(n, i + 1)

                def rounded(u):
                    half, f = divmod(u, FC)
                    cols = slice(half * NH, (half + 1) * NH)
                    wait(act, e_down, e.back(1).times(DOWN, (half + 1) * KC))
                    wait(act, a_gelu, e.times(NU, u + 1))
                    act.activation(hh[:, f, cols], gl[u % 4][:, :], ACT.Copy).then_inc(a_hh, 1)

                for u in range(NU):
                    wait(act, e_up, e.times(NU, u + 1))
                    hold(act, v_hl, e.times(NU, u - 3))
                    act.activation(gl[u % 4][:, :], up_bank[u % 4][:, 0:NH], ACT.Gelu,
                                   bias=biases[:, bass.ds(e.times(FC, u % FC), 1)]).then_inc(a_gelu, 1)
                    if u:
                        rounded(u - 1)
                rounded(NU - 1)
                pieces = iter(range(PIECES))
                for v, count in enumerate((3, 2, 2, 1)):
                    if e1:
                        for _ in range(count):
                            split(e1, next(pieces))
                    half, c = divmod(v, KC)
                    wait(act, e_down, e.times(DOWN, v + 1))
                    hold(act, e_back, e.times(NT))
                    act.activation(yt[:, c, half * NH:(half + 1) * NH], down_bank[v % 2][:, 0:NH], ACT.Identity,
                                   bias=biases[:, bass.ds(e.times(KC, E * FC + c), 1)]).then_inc(a_yt, 1)
                    if e1 and v < TURNS:
                        turned(e1, v)

            steps(act, step)

        @block.tensor
        def _(pe):
            def turn(e, r):
                wait(pe, v_exn, e.times(NT, 2 * r + 2))
                wait(pe, v_xl, e.times(TURNS, r // 2))
                for k in range(KC):
                    for j in range(2):
                        at = (k * 2 + j) * TS
                        last = pe.transpose(turn_bank[r % 2][:, at:at + TS], xn[:, 2 * r + j, k * P:(k + 1) * P],
                                            identf[0:TS, 0:TS])
                last.then_inc(e_turn, 1)

            def back(e, j):
                wait(pe, a_yt, e.times(DOWN, KC * (1 + j // (NT // 2))))
                wait(pe, v_ys, e.times(NT, j - 1))
                if j < 2:
                    wait(pe, a_gelu, e.times(NU, NU))
                for c in range(KC):
                    last = pe.transpose(back_bank[j % 2][0:TS, c * P:(c + 1) * P], yt[:, c, j * TS:(j + 1) * TS],
                                        identf[:, :])
                last.then_inc(e_back, 1)

            for r in range(TURNS - 1):
                turn(expert(0, 0), r)

            def step(n, i):
                e, e0, e1 = expert(n, i), expert(n, i - 1), expert(n, i + 1)
                q = e.slot
                w1 = [w[q][:, 0:KC * F].rearrange("p (k f) -> p k f", k=KC) for w in (wh, wl)]
                w2 = [w[q][:, KC * F:].rearrange("p (c d) -> p c d", c=FC) for w in (wh, wl)]
                xt = [xh[q], xl[q]]
                ht = [hh, hl]
                three = ((0, 0), (0, 1), (1, 0))
                for u in range(NU):
                    half, f = divmod(u, FC)
                    wait(pe, v_xl, e.times(TURNS, TURNS - 1 + half))
                    wait(pe, v_wel, e.times(PIECES, PIECES // 2))
                    wait(pe, a_gelu, e.times(NU, u - 3))
                    if u in (2, 3):
                        wait(pe, v_ys, e.times(NT, u - 3))
                    terms = [(k, a, b) for k in range(KC) for a, b in three]
                    for m, (k, a, b) in enumerate(terms):
                        last = pe.matmul(up_bank[u % 4][:, 0:NH], w1[a][:, k, f * P:(f + 1) * P],
                                         xt[b][:, k, half * NH:(half + 1) * NH],
                                         start=(m == 0), stop=(m == len(terms) - 1))
                    last.then_inc(e_up, 1)
                    if isinstance(n, int) and i == 0 and u == 0:
                        turn(e, TURNS - 1)
                    if e0:
                        for j in ((3, 4), (5,))[u] if u < 2 else ():
                            back(e0, j)
                for v in range(DOWN):
                    half, d = divmod(v, KC)
                    wait(pe, v_hl, e.times(NU, FC * (half + 1)))
                    wait(pe, v_wel, e.times(PIECES, PIECES))
                    wait(pe, a_yt, e.times(DOWN, v - 1))
                    terms = [(c, a, b) for c in range(FC) for a, b in three]
                    for m, (c, a, b) in enumerate(terms):
                        last = pe.matmul(down_bank[v % 2][:, 0:NH], w2[a][:, c, d * P:(d + 1) * P],
                                         ht[b][:, c, half * NH:(half + 1) * NH],
                                         start=(m == 0), stop=(m == len(terms) - 1))
                    last.then_inc(e_down, 1)
                    for j in ((), (), (0, 1), (2,))[v]:
                        back(e, j)
                    if e1 and v < TURNS:
                        turn(e1, v)

            steps(pe, step)
            for j in (3, 4, 5):
                back(expert(0, E - 1), j)

        @block.vector
        def _(dve):
            dve.memset(xs[0][:, :, :], 0.0).then_inc(v_xs0, 1)

            def split(e, c):
                q = e.slot
                wait(dve, a_weh, e.times(PIECES, c + 1))
                dve.tensor_tensor(wl[q][:, c * PC:(c + 1) * PC], raw[q][:, c * PC:(c + 1) * PC],
                                  wh[q][:, c * PC:(c + 1) * PC].bitcast(F32), ALU.subtract).then_inc(v_wel, 1)

            def normalise(e, j):
                rows_of = xs[e.slot]
                wait(dve, d_xs[e.slot][j], e.round(16, 16))
                wait(dve, e_turn, e.times(TURNS))
                dve.tensor_scalar(xn[:, j, :], rows_of[:, j, 0:D], rows_of[:, j, D + 1:D + 2],
                                  rows_of[:, j, D + 2:D + 3], ALU.subtract, ALU.mult).then_inc(v_exn, 1)

            def turned(e, r):
                wait(dve, a_xh, e.times(TURNS, r + 1))
                at = slice(2 * r * TS, 2 * (r + 1) * TS)
                dve.tensor_tensor(xl[e.slot][:, :, at],
                                  turn_bank[r % 2][:, 0:KC * 2 * TS].rearrange("p (k t) -> p k t", k=KC),
                                  xh[e.slot][:, :, at].bitcast(F32), ALU.subtract).then_inc(v_xl, 1)

            e0 = expert(0, 0)
            for c in range(PIECES // 2):
                split(e0, c)
            dve.memset(xs[1][:, :, :], 0.0).then_inc(v_xs0, 1)
            normalise(e0, 0)
            normalise(e0, 1)
            normalise(e0, 2)
            turned(e0, 0)
            normalise(e0, 3)
            turned(e0, 1)
            normalise(e0, 4)
            normalise(e0, 5)
            split(e0, 4)
            turned(e0, 2)
            for c in (5, 6, 7):
                split(e0, c)

            def finish(e, j):
                wait(dve, e_back, e.times(NT, j + 1))
                wait(dve, d_out[j], e.times(16))
                dve.scalar_tensor_tensor(out=ys[j][:, :], in0=back_bank[j % 2][0:TS, 0:D],
                                         scalar=xs[e.slot][:, j, D:D + 1], in1=xs[e.slot][:, j, 0:D],
                                         op0=ALU.mult, op1=ALU.add).then_inc(v_ys, 1)

            def step(n, i):
                e, e0, e1 = expert(n, i), expert(n, i - 1), expert(n, i + 1)
                if e0:
                    for j in (3, 4, 5):
                        finish(e0, j)
                for u in range(NU):
                    half, f = divmod(u, FC)
                    cols = slice(half * NH, (half + 1) * NH)
                    wait(dve, a_hh, e.times(NU, u + 1))
                    dve.tensor_tensor(hl[:, f, cols], gl[u % 4][:, :], hh[:, f, cols].bitcast(F32), ALU.subtract
                                      ).then_inc(v_hl, 1)
                    if e1 and u >= NU - NT:
                        normalise(e1, u - NU + NT)
                pieces = iter(range(PIECES))
                for v, count in enumerate((2, 2, 2, 2)):
                    if e1:
                        for _ in range(count):
                            split(e1, next(pieces))
                    for j in ((), (), (0, 1), (2,))[v]:
                        finish(e, j)
                    if e1 and v < TURNS:
                        turned(e1, v)

            steps(dve, step)
            for j in (3, 4, 5):
                finish(expert(0, E - 1), j)


_INS = ["x", "L0_tok_weight", "L0_attn_q_proj", "L0_attn_k_proj", "L0_attn_v_proj", "L0_attn_o_proj",
        "L0_ffn_wg", "L0_ffn_W1", "L0_ffn_b1", "L0_ffn_W2", "L0_ffn_b2"]


def kernel(**inputs):
    import numpy as _np
    import concourse.bacc as _bacc
    from concourse import mybir as _mybir
    from concourse.bass_utils import run_bass_kernel_spmd as _run

    nc = _bacc.Bacc("TRN2", target_bir_lowering=False, num_devices=1)
    arrays, args = {}, []
    for name in _INS:
        a = _np.ascontiguousarray(inputs[name])
        arrays[f"in_{name}_dram"] = a
        args.append(nc.dram_tensor(f"in_{name}_dram", a.shape, _mybir.dt.from_np(a.dtype), kind="ExternalInput").ap())
    nb, s = inputs["x"].shape
    d = inputs["L0_tok_weight"].shape[1]
    args.append(nc.dram_tensor("out_0_dram", (nb, s, d), _mybir.dt.float32, kind="ExternalOutput").ap())
    lm_block(nc, *args)
    r = _run(nc, [arrays], core_ids=[0])
    return r.results[0]["out_0_dram"]
```
